# Optimizing a Trainium2 kernel written in Bass

```python
import numpy as np
import jax
import jax.numpy as jnp

def _softmax(x, axis=-1):
    return jax.nn.softmax(x, axis=axis)

def _gelu(x):
    return jax.nn.gelu(x, approximate=True)

def _silu(x):
    return jax.nn.silu(x)

def _sigmoid(x):
    return jax.nn.sigmoid(x)

def _layernorm(x, axis=-1, eps=1e-05):
    m = jnp.mean(x, axis=axis, keepdims=True)
    v = jnp.var(x, axis=axis, keepdims=True)
    return (x - m) / jnp.sqrt(v + eps)

def _scatter_add(tgt, idx, src, axis=0):
    return tgt.at[idx].add(src)

def _segment_sum(src, seg, n):
    return jax.ops.segment_sum(src, seg, n)
kernel_name = 'mk_gnn_ffn_d1_gnn_r8_bdd047'

def setup_inputs(seed: int=0):
    np.random.seed(seed)
    _w = jnp.asarray

    def _rec_inputs():
        import jax
        import jax.numpy as jnp
        _gk = jax.random.key(seed)
        x = -6.415e-05 + 1 * jax.random.normal(jax.random.fold_in(_gk, 1), (6250, 512), jnp.float32)
        _s = jax.random.randint(jax.random.fold_in(_gk, 2), (50000,), 0, 6250, jnp.int32)
        _d = jax.random.randint(jax.random.fold_in(_gk, 3), (50000,), 0, 6250, jnp.int32)
        _loop = jnp.arange(6250, dtype=jnp.int32)
        src = jnp.concatenate([_s, _d, _loop])
        dst = jnp.concatenate([_d, _s, _loop])
        _o = jnp.argsort(dst, stable=True)
        src = src[_o]
        dst = dst[_o]
        return (x, src, dst)
    x, src, dst = _rec_inputs()

    def _L0_gnn_setup():
        import jax, jax.numpy as jnp
        import numpy as np
        N = 2500
        E = 40000
        LN_EPS = 1e-05
        NEG_SLOPE = 0.2

        def _segment_softmax(logits, seg, num_segments):
            m = jax.ops.segment_max(logits, seg, num_segments=num_segments)
            e = jnp.exp(logits - m[seg])
            s = jax.ops.segment_sum(e, seg, num_segments=num_segments)
            return e / s[seg]

        def _gat_conv(x, src, dst, W, a_s, a_d, b, concat):
            H, C = a_s.shape
            n = x.shape[0]
            h = (x @ W).reshape(n, H, C)
            alpha_s = jnp.einsum('nhc,hc->nh', h, a_s)
            alpha_d = jnp.einsum('nhc,hc->nh', h, a_d)
            logits = jax.nn.leaky_relu(alpha_s[src] + alpha_d[dst], NEG_SLOPE)
            alpha = _segment_softmax(logits, dst, n)
            msg = h[src] * alpha[:, :, None]
            out = jax.ops.segment_sum(msg, dst, num_segments=n)
            out = out.reshape(n, H * C) if concat else out.mean(axis=1)
            return out + b

        def _layer_norm(x, g, beta):
            mu = jnp.mean(x, axis=-1, keepdims=True)
            var = jnp.var(x, axis=-1, keepdims=True)
            return (x - mu) * jax.lax.rsqrt(var + LN_EPS) * g + beta

        def _forward(x, edge_index, W1, a_src1, a_dst1, b1, g1, beta1, W2, a_src2, a_dst2, b2, g2, beta2):
            n = x.shape[0]
            loops = jnp.arange(n, dtype=edge_index.dtype)
            src = jnp.concatenate([edge_index[0], loops])
            dst = jnp.concatenate([edge_index[1], loops])
            x_new = _gat_conv(x, src, dst, W1, a_src1, a_dst1, b1, concat=True)
            x_new = jax.nn.elu(_layer_norm(x_new, g1, beta1))
            x = x + x_new
            x_new = _gat_conv(x, src, dst, W2, a_src2, a_dst2, b2, concat=False)
            x_new = jax.nn.elu(_layer_norm(x_new, g2, beta2))
            return x + x_new
        key = jax.random.key(seed)
        ks = jax.random.split(key, 12)
        d = {}
        d['x'] = jax.random.normal(ks[0], (N, 512), dtype=jnp.float32)
        d['edge_index'] = jax.random.randint(ks[1], (2, E), 0, N, dtype=jnp.int64)
        s = 1.0 / np.sqrt(512.0)
        d['W1'] = jax.random.normal(ks[2], (512, 512), dtype=jnp.float32) * s
        d['a_src1'] = jax.random.normal(ks[3], (8, 64), dtype=jnp.float32) * s
        d['a_dst1'] = jax.random.normal(ks[4], (8, 64), dtype=jnp.float32) * s
        d['b1'] = jnp.zeros((512,), jnp.float32)
        d['g1'] = jnp.ones((512,), jnp.float32)
        d['beta1'] = jnp.zeros((512,), jnp.float32)
        d['W2'] = jax.random.normal(ks[5], (512, 512), dtype=jnp.float32) * s
        d['a_src2'] = jax.random.normal(ks[6], (1, 512), dtype=jnp.float32) * s
        d['a_dst2'] = jax.random.normal(ks[7], (1, 512), dtype=jnp.float32) * s
        d['b2'] = jnp.zeros((512,), jnp.float32)
        d['g2'] = jnp.ones((512,), jnp.float32)
        d['beta2'] = jnp.zeros((512,), jnp.float32)
        return d
    _L0_gnn_all = _L0_gnn_setup()
    _L0_gnn_in = {k: v for k, v in _L0_gnn_all.items() if k in ('W1', 'a_src1', 'a_dst1', 'b1', 'g1', 'beta1', 'W2', 'a_src2', 'a_dst2', 'b2', 'g2', 'beta2')}
    del _L0_gnn_all

    def _L0_ffn_setup():
        import jax, jax.numpy as jnp
        import numpy as np
        B, S, H, E, K, DF, SH = (8, 512, 512, 8, 2, 128, 512)
        key = jax.random.key(seed)
        ks = jax.random.split(key, 10)
        n = lambda i, shape, sc: jax.random.normal(ks[i], shape, jnp.float32) * sc
        return {'hidden_states': n(0, (B, S, H), 1.0), 'gate_w': n(1, (E, H), 0.05), 'w1': n(2, (E, H, DF), 0.05), 'b1': n(3, (E, DF), 0.01), 'w2': n(4, (E, DF, H), 0.05), 'b2': n(5, (E, H), 0.01), 'sw1': n(6, (H, SH), 0.05), 'sb1': n(7, (SH,), 0.01), 'sw2': n(8, (SH, H), 0.05), 'sb2': n(9, (H,), 0.01)}
    _L0_ffn_all = _L0_ffn_setup()
    _L0_ffn_in = {k: v for k, v in _L0_ffn_all.items() if k in ('gate_w', 'w1', 'b1', 'w2', 'b2', 'sw1', 'sb1', 'sw2', 'sb2')}
    del _L0_ffn_all
    return {'x': x, 'src': src, 'dst': dst, 'L0_gnn_W1': _L0_gnn_in['W1'], 'L0_gnn_a_src1': _L0_gnn_in['a_src1'], 'L0_gnn_a_dst1': _L0_gnn_in['a_dst1'], 'L0_gnn_b1': _L0_gnn_in['b1'], 'L0_gnn_g1': _L0_gnn_in['g1'], 'L0_gnn_beta1': _L0_gnn_in['beta1'], 'L0_gnn_W2': _L0_gnn_in['W2'], 'L0_gnn_a_src2': _L0_gnn_in['a_src2'], 'L0_gnn_a_dst2': _L0_gnn_in['a_dst2'], 'L0_gnn_b2': _L0_gnn_in['b2'], 'L0_gnn_g2': _L0_gnn_in['g2'], 'L0_gnn_beta2': _L0_gnn_in['beta2'], 'L0_ffn_gate_w': _L0_ffn_in['gate_w'], 'L0_ffn_w1': _L0_ffn_in['w1'], 'L0_ffn_b1': _L0_ffn_in['b1'], 'L0_ffn_w2': _L0_ffn_in['w2'], 'L0_ffn_b2': _L0_ffn_in['b2'], 'L0_ffn_sw1': _L0_ffn_in['sw1'], 'L0_ffn_sb1': _L0_ffn_in['sb1'], 'L0_ffn_sw2': _L0_ffn_in['sw2'], 'L0_ffn_sb2': _L0_ffn_in['sb2']}

def reference(x, src, dst, L0_gnn_W1, L0_gnn_a_src1, L0_gnn_a_dst1, L0_gnn_b1, L0_gnn_g1, L0_gnn_beta1, L0_gnn_W2, L0_gnn_a_src2, L0_gnn_a_dst2, L0_gnn_b2, L0_gnn_g2, L0_gnn_beta2, L0_ffn_gate_w, L0_ffn_w1, L0_ffn_b1, L0_ffn_w2, L0_ffn_b2, L0_ffn_sw1, L0_ffn_sb1, L0_ffn_sw2, L0_ffn_sb2):
    import jax
    import jax.numpy as jnp

    def _L0_gnn_ref(x, edge_index, W1, a_src1, a_dst1, b1, g1, beta1, W2, a_src2, a_dst2, b2, g2, beta2):
        import jax, jax.numpy as jnp
        import numpy as np
        N = 2500
        E = 40000
        LN_EPS = 1e-05
        NEG_SLOPE = 0.2

        def _segment_softmax(logits, seg, num_segments):
            m = jax.ops.segment_max(logits, seg, num_segments=num_segments)
            e = jnp.exp(logits - m[seg])
            s = jax.ops.segment_sum(e, seg, num_segments=num_segments)
            return e / s[seg]

        def _gat_conv(x, src, dst, W, a_s, a_d, b, concat):
            H, C = a_s.shape
            n = x.shape[0]
            h = (x @ W).reshape(n, H, C)
            alpha_s = jnp.einsum('nhc,hc->nh', h, a_s)
            alpha_d = jnp.einsum('nhc,hc->nh', h, a_d)
            logits = jax.nn.leaky_relu(alpha_s[src] + alpha_d[dst], NEG_SLOPE)
            alpha = _segment_softmax(logits, dst, n)
            msg = h[src] * alpha[:, :, None]
            out = jax.ops.segment_sum(msg, dst, num_segments=n)
            out = out.reshape(n, H * C) if concat else out.mean(axis=1)
            return out + b

        def _layer_norm(x, g, beta):
            mu = jnp.mean(x, axis=-1, keepdims=True)
            var = jnp.var(x, axis=-1, keepdims=True)
            return (x - mu) * jax.lax.rsqrt(var + LN_EPS) * g + beta

        def _forward(x, edge_index, W1, a_src1, a_dst1, b1, g1, beta1, W2, a_src2, a_dst2, b2, g2, beta2):
            n = x.shape[0]
            loops = jnp.arange(n, dtype=edge_index.dtype)
            src = jnp.concatenate([edge_index[0], loops])
            dst = jnp.concatenate([edge_index[1], loops])
            x_new = _gat_conv(x, src, dst, W1, a_src1, a_dst1, b1, concat=True)
            x_new = jax.nn.elu(_layer_norm(x_new, g1, beta1))
            x = x + x_new
            x_new = _gat_conv(x, src, dst, W2, a_src2, a_dst2, b2, concat=False)
            x_new = jax.nn.elu(_layer_norm(x_new, g2, beta2))
            return x + x_new
        return _forward(x, edge_index, W1, a_src1, a_dst1, b1, g1, beta1, W2, a_src2, a_dst2, b2, g2, beta2)

    def _L0_ffn_ref(hidden_states, gate_w, w1, b1, w2, b2, sw1, sb1, sw2, sb2):
        import jax, jax.numpy as jnp
        import numpy as np
        B, S, H, E, K, DF, SH = (8, 512, 512, 8, 2, 128, 512)
        x = hidden_states
        xf = x.reshape(-1, x.shape[-1])
        T = xf.shape[0]
        scores = jax.nn.softmax(xf @ gate_w.T, axis=-1)
        topk_w, topk_i = jax.lax.top_k(scores, K)
        topk_w = topk_w / (topk_w.sum(-1, keepdims=True) + 1e-20)
        combine = jnp.zeros((T, E), xf.dtype).at[jnp.arange(T)[:, None], topk_i].add(topk_w)
        h1 = jax.nn.relu(jnp.einsum('th,ehf->tef', xf, w1) + b1)
        eo = jnp.einsum('tef,efh->teh', h1, w2) + b2
        y = jnp.einsum('te,teh->th', combine, eo)
        shared = jax.nn.relu(xf @ sw1 + sb1) @ sw2 + sb2
        return (y + shared).reshape(x.shape)
    edge_index = jnp.stack([src, dst])
    x = x + _L0_gnn_ref(_layernorm(x, axis=-1), edge_index, L0_gnn_W1, L0_gnn_a_src1, L0_gnn_a_dst1, L0_gnn_b1, L0_gnn_g1, L0_gnn_beta1, L0_gnn_W2, L0_gnn_a_src2, L0_gnn_a_dst2, L0_gnn_b2, L0_gnn_g2, L0_gnn_beta2)
    x = x + _L0_ffn_ref(_layernorm(x, axis=-1)[None], L0_ffn_gate_w, L0_ffn_w1, L0_ffn_b1, L0_ffn_w2, L0_ffn_b2, L0_ffn_sw1, L0_ffn_sb1, L0_ffn_sw2, L0_ffn_sb2)[0]
    return x

_drawn_inputs = setup_inputs


def setup_inputs(seed=0):
    import zlib

    import numpy as np

    out = dict(_drawn_inputs(seed))
    spreads = {'L0_gnn_b1': (0.0, 0.1),
     'L0_gnn_g1': (1.0, 0.2),
     'L0_gnn_beta1': (0.0, 0.1),
     'L0_gnn_b2': (0.0, 0.1),
     'L0_gnn_g2': (1.0, 0.2),
     'L0_gnn_beta2': (0.0, 0.1)}
    factors = {'L0_ffn_b1': 50.441, 'L0_ffn_b2': 8.0, 'L0_ffn_sb1': 8.0, 'L0_ffn_sb2': 8.0}
    for name, (base, spread) in spreads.items():
        noise = np.random.default_rng([zlib.crc32(name.encode()), seed]).standard_normal(out[name].shape)
        drawn = base * np.exp(spread * noise) if base else spread * noise
        out[name] = jnp.asarray(drawn.astype(out[name].dtype))
    for name, factor in factors.items():
        out[name] = (out[name] * factor).astype(out[name].dtype)
    return out
```

```python
from contextlib import ExitStack

import concourse.bass as bass
from concourse import mybir

ALU = mybir.AluOpType
ACT = mybir.ActivationFunctionType
AX = mybir.AxisListType
F32 = mybir.dt.float32
I32 = mybir.dt.int32
BF16 = mybir.dt.bfloat16

P = 128
D = 512
KT = D // P
EPS = 1e-5
SLOPE = 0.2
MAGIC_MINUS = float(0x5F3759DF - (1 << 31) - (1 << 22))
OUTSIDE = 30000.0


class Steps:

    def __init__(self, eng, sem, base=0):
        self.eng, self.sem, self.base, self.n = eng, sem, base, 0

    def link(self, ins):
        self.n += 1
        ins.then_inc(self.sem, 1)
        self.eng.wait_ge(self.sem, self.base + self.n)


def need(eng, sem, n):
    if not isinstance(n, int) or n > 0:
        eng.wait_ge(sem, n)


def gnn_ffn(nc, x, src, dst, W1, a_src1, a_dst1, b1, g1, beta1, W2, a_src2, a_dst2, b2, g2, beta2,
            gate_w, w1, fb1, w2, fb2, sw1, sb1, sw2, sb2, out):
    N = x.shape[0]
    E = src.shape[0]
    H = a_src1.shape[0]
    C = D // H
    NE = gate_w.shape[0]
    NT = -(-N // P)
    LAST = N - (NT - 1) * P
    CG = -(-(E + P) // (P * P))
    CH = P * CG
    NCH = -(-E // P)
    RING = 16
    QMAX = -(-(NCH + NT + 3 * NT) // RING) * 4
    VG = -(-4 * (QMAX + 2) // P)
    QG = -(-(QMAX + 2) // P)
    RW = D + 8
    FG = 3
    assert NCH < CH and LAST > 0 and C * H == D and NE == 8

    with ExitStack() as ctx:
        def sb(name, shape, dt=F32):
            return ctx.enter_context(nc.sbuf_tensor(name, shape, dt))

        def sem(name):
            return ctx.enter_context(nc.semaphore(name))

        banks = [ctx.enter_context(nc.psum_tensor(f"bank{i}", [P, 512], F32)) for i in range(8)]
        acc_ps, nodes_ps, tr_ps, dense_ps, hid0_ps, hid1_ps, crep_ps, small_ps = banks

        edge_tab = nc.dram_tensor("edge_tab", (CH, 2 * P), F32).ap()
        rel_tab = nc.dram_tensor("rel_tab", (VG * P, P), BF16).ap()
        h_tab = [nc.dram_tensor(f"h_tab{i}", (N, RW), F32).ap() for i in (1, 2)]
        x1_tab = nc.dram_tensor("x1_tab", (N, D), F32).ap()

        acc_tab = nc.dram_tensor("acc_tab", (NT * P, RW), F32).ap()

        ident = sb("ident", [P, P])
        iota_n = sb("iota_n", [P, P])
        iota_p = sb("iota_p", [P, 1])
        ones = sb("ones", [P, P])
        zero_b = sb("zero_b", [P, 512], BF16)
        less = sb("less", [P, NE, NE])
        relN = sb("relN", [P, VG * P])
        srcT = sb("srcT", [P, VG * P], I32)
        quad_tile = sb("quad_tile", [1, QG * P], I32)
        q_end = sb("q_end", [P, NT + 2], I32)
        Wc = [sb("W1s", [P, KT, D]), sb("W2s", [P, KT, D])]
        WA = [sb("WA1", [P, KT, 16]), sb("WA2", [P, KT, 16])]
        vecs = sb("vecs", [P, 6, D])
        sw1_s = sb("sw1_s", [P, KT, D])
        w1_s = sb("w1_s", [P, KT, NE, P])
        sw2_s = sb("sw2_s", [P, KT, D])
        w2_s = sb("w2_s", [P, NE, D])
        gateT = sb("gateT", [P, KT, NE])
        hb = sb("hb", [P, 12])
        b2c = sb("b2c", [NE + 1, D])
        sel = sb("sel", [NE + 1, NE, P])
        AS = sb("AS", [P, NT, 8])
        AD = sb("AD", [P, NT, 8])
        NRb = sb("NRb", [P, NT, 3, 16], BF16)
        ES = sb("ES", [P, NT, 8])
        amax = sb("amax", [P, 8])
        amaxp = sb("amaxp", [P, 8])
        stats = sb("stats", [P, NT, 2])
        sm = sb("sm", [P, 32])
        bn = sb("bn", [P, 6])

        def tile_rows(tab, t, n=P):
            return tab[bass.ds(t * P, n), :] if n == P else tab[(NT - 1) * P:N, :]

        def setup_stage():
            dstage = ctx_stage.enter_context(nc.sbuf_tensor("dstage", [P, CG * P], I32))
            sstage = ctx_stage.enter_context(nc.sbuf_tensor("sstage", [P, CG * P], I32))
            et = ctx_stage.enter_context(nc.sbuf_tensor("et", [P, CG, 2 * P], F32))
            vt = ctx_stage.enter_context(nc.sbuf_tensor("vt", [P, VG, 2 * P], F32))
            cnt = ctx_stage.enter_context(nc.sbuf_tensor("cnt", [P, 64], F32))
            f = [ctx_stage.enter_context(nc.sbuf_tensor(f"f{i}", [P, 64], F32)) for i in range(8)]
            n_i = [ctx_stage.enter_context(nc.sbuf_tensor(f"n{i}", [P, 64], I32)) for i in range(4)]
            big = ctx_stage.enter_context(nc.sbuf_tensor("big", [P, VG, NT], F32))
            big2 = ctx_stage.enter_context(nc.sbuf_tensor("big2", [P, VG, NT], F32))
            big3 = ctx_stage.enter_context(nc.sbuf_tensor("big3", [P, QG, NT], F32))
            qt = ctx_stage.enter_context(nc.sbuf_tensor("qt", [P, QG], F32))
            qdiag = ctx_stage.enter_context(nc.sbuf_tensor("qdiag", [P, QG * P], F32))
            relb = ctx_stage.enter_context(nc.sbuf_tensor("relb", [P, VG, P], BF16))
            vnum = ctx_stage.enter_context(nc.sbuf_tensor("vnum", [P, VG], F32))
            vt_t = ctx_stage.enter_context(nc.sbuf_tensor("vt_t", [P, VG], F32))
            vt_c = ctx_stage.enter_context(nc.sbuf_tensor("vt_c", [P, VG], F32))
            vt_o = ctx_stage.enter_context(nc.sbuf_tensor("vt_o", [P, VG], F32))
            vt_ci = ctx_stage.enter_context(nc.sbuf_tensor("vt_ci", [P, VG], I32))
            junk = ctx_stage.enter_context(nc.sbuf_tensor("junk", [P, CG * P], F32))
            ab = ctx_stage.enter_context(nc.sbuf_tensor("ab", [P, 4, D], F32))
            gnat = ctx_stage.enter_context(nc.sbuf_tensor("gnat", [NE, D], F32))
            hbn = ctx_stage.enter_context(nc.sbuf_tensor("hbn", [12, P], F32))
            prod = ctx_stage.enter_context(nc.sbuf_tensor("prod", [P, D], F32))
            s_pads, s_edges, s_const, s_et, s_etout = (sem(n) for n in (
                "edge_pads_set", "edges_loaded", "constants_made", "edge_table_made", "edge_table_stored"))
            s_w, s_dve, s_cnt, s_cntps, s_vidx, s_vg, s_rel, s_relout, s_tr, s_trc, s_wt = (sem(n) for n in (
                "weights_loaded", "setup_vector_steps", "counts_made", "counts_summed", "visit_chunks_known",
                "visits_gathered", "visit_rows_made", "visit_rows_stored", "visit_transposed",
                "visit_copied", "gate_transposed"))
            s_tile = sem("visit_tiles_known")
            s_ab = sem("attention_vectors_loaded")
            full = E // (CG * P)
            rest = E - full * CG * P
            NVEC = 6
            vec_in = [b1, g1, beta1, b2, g2, beta2]
            ab_in = [a_src1.rearrange("h c -> (h c)"), a_dst1.rearrange("h c -> (h c)"),
                     a_src2.rearrange("h c -> (h c)"), a_dst2.rearrange("h c -> (h c)")]

            with nc.Block() as block:
                @block.sync
                def _(sp):
                    sp.wait_ge(s_pads, 2)
                    for stage, arr in ((dstage, dst), (sstage, src)):
                        sp.dma_start(stage[0:full, :], arr[0:full * CG * P].rearrange("(p k) -> p k", k=CG * P)).then_inc(s_edges, 16)
                        sp.dma_start(stage[full:full + 1, 0:rest], arr[full * CG * P:E].rearrange("(a k) -> a k", a=1)).then_inc(s_edges, 16)
                    for i, a in enumerate(ab_in):
                        sp.dma_start(ab[:, i, :], a.rearrange("(a k) -> a k", a=1).to_broadcast([P, D])).then_inc(s_ab, 16)
                    for w, dest in ((W1, Wc[0]), (W2, Wc[1])):
                        sp.dma_start(dest[:], w.rearrange("(k p) n -> p k n", p=P)).then_inc(s_ab, 16)
                    sp.dma_start(gnat[:], gate_w).then_inc(s_w, 16)
                    sp.dma_start(hbn[0:4, :], sb1.rearrange("(k p) -> k p", p=P)).then_inc(s_w, 16)
                    sp.dma_start(hbn[4:12, :], fb1).then_inc(s_w, 16)
                    sp.dma_start(sw1_s[:], sw1.rearrange("(k p) n -> p k n", p=P)).then_inc(s_w, 16)
                    sp.dma_start(sw2_s[:], sw2.rearrange("(k p) n -> p k n", p=P)).then_inc(s_w, 16)
                    sp.dma_start(w2_s[:], w2.rearrange("e p n -> p e n")).then_inc(s_w, 16)
                    for k in range(KT):
                        sp.dma_start(w1_s[:, k], w1[:, k * P:(k + 1) * P, :].rearrange("e p n -> p e n")).then_inc(s_w, 16)
                    sp.dma_start(b2c[0:NE, :], fb2).then_inc(s_w, 16)
                    sp.dma_start(b2c[NE:NE + 1, :], sb2.rearrange("(a k) -> a k", a=1)).then_inc(s_w, 16)
                    for i, a in enumerate(vec_in):
                        sp.dma_start(vecs[:, i, :], a.rearrange("(a k) -> a k", a=1).to_broadcast([P, D])).then_inc(s_w, 16)
                    sp.wait_ge(s_w, 16 * (12 + NVEC))
                    sp.wait_ge(s_ab, 16 * 6)

                @block.gpsimd
                def _(pool):
                    nc.gpsimd.memset(ones[:], 1.0).then_inc(s_const, 1)
                    nc.gpsimd.memset(zero_b[:], 0.0).then_inc(s_const, 1)
                    nc.gpsimd.iota(iota_n[:], pattern=[[-1, P]], base=0, channel_multiplier=0, allow_small_or_imprecise_dtypes=True).then_inc(s_const, 1)
                    nc.gpsimd.iota(iota_p[:], pattern=[[0, 1]], base=0, channel_multiplier=1, allow_small_or_imprecise_dtypes=True).then_inc(s_const, 1)
                    nc.gpsimd.iota(vnum[:], pattern=[[P, VG]], base=0, channel_multiplier=1, allow_small_or_imprecise_dtypes=True).then_inc(s_const, 1)
                    pool.wait_ge(s_const, 5)
                    nc.gpsimd.affine_select(out=ident[:], in_=ones[:], compare_op=ALU.is_equal, fill=0.0, base=0, pattern=[[1, P]], channel_multiplier=-1).then_inc(s_const, 1)
                    nc.gpsimd.affine_select(out=sel[:], in_=ones[0:NE + 1, :].rearrange("p (a k) -> p a k", a=1).to_broadcast([NE + 1, NE, P]), compare_op=ALU.is_equal, fill=0.0, base=0, pattern=[[1, NE], [0, P]], channel_multiplier=-1).then_inc(s_const, 1)
                    nc.gpsimd.affine_select(out=less[:], in_=ones[:, 0:NE * NE].rearrange("p (a k) -> p a k", a=NE), compare_op=ALU.is_gt, fill=0.0, base=0, pattern=[[1, NE], [-1, NE]], channel_multiplier=0).then_inc(s_const, 1)
                    pool.wait_ge(s_etout, 16)
                    pool.wait_ge(s_vidx, 1)
                    for k in range(VG):
                        nc.gpsimd.indirect_dma_start(vt[:, k, :], None, edge_tab, bass.IndirectOffsetOnAxis(ap=vt_ci[:, k:k + 1], axis=0)).then_inc(s_vg, 16)

                @block.vector
                def _(dve):
                    st = Steps(dve, s_dve)
                    v = nc.vector
                    v.memset(dstage[:], int(OUTSIDE)).then_inc(s_pads, 1)
                    v.memset(sstage[:], 0).then_inc(s_pads, 1)
                    dve.wait_ge(s_edges, 64)
                    df = et[:, :, 0:P]
                    v.tensor_copy(et[:, :, P:2 * P], sstage[:].rearrange("p (c k) -> p c k", k=P)).then_inc(s_et, 1)
                    st.link(v.tensor_copy(df, dstage[:].rearrange("p (c k) -> p c k", k=P)))
                    dve.sem_inc(s_et, 1)
                    for t in range(1, NT + 1):
                        v.tensor_scalar(junk[:].rearrange("p (c k) -> p c k", k=P), df, float(P * t), 0.0, ALU.is_lt, ALU.add, accum_out=cnt[:, t:t + 1]).then_inc(s_cnt, 1)
                        dve.wait_ge(s_cnt, t)
                    v.memset(cnt[:, 0:1], 0.0).then_inc(s_cnt, 1)
                    dve.wait_ge(s_cntps, 1)
                    first, c0, last_, c1, nvis, nquad, qe, dd = f
                    T1 = NT + 1
                    st.link(v.tensor_copy(first[:, 0:T1], small_ps[:, 0:T1]))
                    st.link(v.tensor_copy(n_i[0][:, 0:T1], first[:, 0:T1]))
                    st.link(v.tensor_scalar(last_[:, 0:NT], first[:, 1:T1], -1.0, None, ALU.add))
                    st.link(v.tensor_copy(n_i[1][:, 0:NT], last_[:, 0:NT]))
                    st.link(v.tensor_single_scalar(n_i[2][:, 0:T1], n_i[0][:, 0:T1], 7, ALU.arith_shift_right))
                    st.link(v.tensor_single_scalar(n_i[3][:, 0:NT], n_i[1][:, 0:NT], 7, ALU.arith_shift_right))
                    st.link(v.tensor_copy(c0[:, 0:T1], n_i[2][:, 0:T1]))
                    st.link(v.tensor_copy(c1[:, 0:NT], n_i[3][:, 0:NT]))
                    st.link(v.tensor_tensor(nvis[:, 0:NT], c1[:, 0:NT], c0[:, 0:NT], ALU.subtract))
                    st.link(v.tensor_scalar(nvis[:, 0:NT], nvis[:, 0:NT], 1.0, 1.0, ALU.add, ALU.max))
                    st.link(v.tensor_scalar(nvis[:, 0:NT], nvis[:, 0:NT], 3.0, None, ALU.add))
                    st.link(v.tensor_copy(n_i[0][:, 0:NT], nvis[:, 0:NT]))
                    st.link(v.tensor_single_scalar(n_i[1][:, 0:NT], n_i[0][:, 0:NT], 2, ALU.arith_shift_right))
                    st.link(v.tensor_copy(nquad[:, 0:NT], n_i[1][:, 0:NT]))
                    st.link(v.memset(qe[:], 0.0))
                    st.link(v.memset(last_[:], 0.0))
                    st.link(v.tensor_tensor_scan(qe[:, 1:T1], nquad[:, 0:NT], last_[:, 0:NT], 0.0, ALU.add, ALU.add))
                    st.link(v.tensor_scalar(first[:, 0:1], qe[:, NT:T1], 3.0, None, ALU.add))
                    st.link(v.tensor_copy(n_i[0][:, 0:1], first[:, 0:1]))
                    st.link(v.tensor_single_scalar(n_i[1][:, 0:1], n_i[0][:, 0:1], 2, ALU.arith_shift_right))
                    st.link(v.tensor_copy(first[:, 0:1], n_i[1][:, 0:1]))
                    st.link(v.tensor_scalar(qe[:, NT:T1], first[:, 0:1], 4.0, None, ALU.mult))
                    st.link(v.tensor_copy(q_end[:, 0:T1], qe[:, 0:T1]))
                    st.link(v.tensor_copy(q_end[:, T1:T1 + 1], first[:, 0:1]))
                    dve.wait_ge(s_const, 5)
                    st.link(v.tensor_tensor(big3[:, :, 0:NT - 1], vnum[:, 0:QG].rearrange("p (v a) -> p v a", a=1).to_broadcast([P, QG, NT - 1]),
                                            qe[:, 1:NT].rearrange("p (a t) -> p a t", a=1).to_broadcast([P, QG, NT - 1]), ALU.is_ge))
                    st.link(v.tensor_reduce(qt[:], big3[:, :, 0:NT - 1], AX.X, ALU.add))
                    dve.wait_ge(s_const, 6)
                    for k in range(QG):
                        v.tensor_scalar(qdiag[:, k * P:(k + 1) * P], ident[:], qt[:, k:k + 1], None, ALU.mult).then_inc(s_tile, 1)
                    st.link(v.tensor_scalar(qe[:, 0:T1], qe[:, 0:T1], 4.0, None, ALU.mult))
                    st.link(v.tensor_tensor(dd[:, 0:NT], c0[:, 0:NT], qe[:, 0:NT], ALU.subtract))
                    st.link(v.tensor_tensor(nvis[:, 1:NT], dd[:, 1:NT], dd[:, 0:NT - 1], ALU.subtract))
                    vb = vnum[:].rearrange("p (v a) -> p v a", a=1).to_broadcast([P, VG, NT - 1])
                    qb = qe[:, 1:NT].rearrange("p (a t) -> p a t", a=1).to_broadcast([P, VG, NT - 1])
                    db = nvis[:, 1:NT].rearrange("p (a t) -> p a t", a=1).to_broadcast([P, VG, NT - 1])
                    st.link(v.tensor_tensor(big[:, :, 0:NT - 1], vb, qb, ALU.is_ge))
                    st.link(v.tensor_reduce(vt_t[:], big[:, :, 0:NT - 1], AX.X, ALU.add))
                    st.link(v.tensor_tensor(big2[:, :, 0:NT - 1], big[:, :, 0:NT - 1], db, ALU.mult))
                    st.link(v.tensor_reduce(vt_c[:], big2[:, :, 0:NT - 1], AX.X, ALU.add))
                    st.link(v.tensor_tensor(vt_c[:], vt_c[:], vnum[:], ALU.add))
                    st.link(v.tensor_scalar(vt_c[:], vt_c[:], 0.0, float(NCH), ALU.max, ALU.min))
                    v.tensor_copy(vt_ci[:], vt_c[:]).then_inc(s_vidx, 1)
                    st.link(v.tensor_scalar(vt_o[:], vt_t[:], -float(P), None, ALU.mult))
                    dve.wait_ge(s_tr, 1)
                    st.link(v.tensor_copy(quad_tile[:], hid0_ps[0:1, 0:QG * P]))
                    dve.wait_ge(s_vg, 16 * VG)
                    for k in range(VG):
                        v.tensor_scalar(vt[:, k, 0:P], vt[:, k, 0:P], vt_o[:, k:k + 1], None, ALU.add).then_inc(s_rel, 1)
                    dve.wait_ge(s_rel, VG)
                    v.tensor_copy(relb[:], vt[:, :, 0:P]).then_inc(s_rel, 1)
                    for k in range(VG):
                        dve.wait_ge(s_trc, k + 1)
                        v.tensor_scalar(relN[:, k * P:(k + 1) * P], (tr_ps, dense_ps)[k % 2][:, 0:P], -1.0, None, ALU.mult).then_inc(s_cnt, 1)
                        v.tensor_copy(srcT[:, k * P:(k + 1) * P], (tr_ps, dense_ps)[k % 2][:, P:2 * P]).then_inc(s_cnt, 1)
                    dve.wait_ge(s_ab, 96)
                    for i in range(2):
                        nh = (H, 1)[i]
                        for k in range(KT):
                            for j in range(2):
                                st.link(v.tensor_tensor(prod[:], Wc[i][:, k, :], ab[:, 2 * i + j, :], ALU.mult))
                                st.link(v.tensor_reduce(WA[i][:, k, j * nh:(j + 1) * nh], prod[:].rearrange("p (h c) -> p h c", h=nh), AX.X, ALU.add))
                    dve.wait_ge(s_wt, 1)
                    st.link(v.tensor_copy(gateT[:], acc_ps[:, 0:KT * NE].rearrange("p (k e) -> p k e", k=KT)))
                    st.link(v.tensor_copy(hb[:], nodes_ps[:, 0:12]))

                @block.scalar
                def _(act):
                    act.wait_ge(s_et, 2)
                    act.dma_start(edge_tab.rearrange("(p c) k -> p c k", c=CG), et[:]).then_inc(s_etout, 16)
                    act.wait_ge(s_rel, VG + 1)
                    act.dma_start(rel_tab.rearrange("(k p) e -> p k e", p=P), relb[:]).then_inc(s_relout, 16)
                    act.wait_ge(s_relout, 16)

                @block.tensor
                def _(pe):
                    m = nc.tensor
                    pe.wait_ge(s_cnt, NT + 1)
                    pe.wait_ge(s_const, 8)
                    m.matmul(small_ps[:, 0:NT + 1], ones[:], cnt[:, 0:NT + 1], start=True, stop=True).then_inc(s_cntps, 1)
                    pe.wait_ge(s_tile, QG)
                    m.matmul(hid0_ps[:, 0:QG * P], ones[:], qdiag[:], start=True, stop=True).then_inc(s_tr, 1)
                    pe.wait_ge(s_rel, VG)
                    for k in range(VG):
                        bank = (tr_ps, dense_ps)[k % 2]
                        if k >= 2:
                            pe.wait_ge(s_cnt, NT + 1 + 2 * (k - 1))
                        m.transpose(bank[:, 0:P], vt[:, k, 0:P], ident[:])
                        m.transpose(bank[:, P:2 * P], vt[:, k, P:2 * P], ident[:]).then_inc(s_trc, 1)
                    pe.wait_ge(s_w, 16 * (12 + NVEC))
                    for k in range(KT):
                        m.transpose(acc_ps[:, k * NE:(k + 1) * NE], gnat[:, k * P:(k + 1) * P], ident[0:NE, 0:NE])
                    m.transpose(nodes_ps[:, 0:12], hbn[:], ident[0:12, 0:12]).then_inc(s_wt, 1)

        def rsqrt_steps(st, var, o):
            v = nc.vector
            half, y, t1 = (sm[:, o + i:o + i + 1] for i in range(3))
            st.link(v.tensor_scalar(half, var, EPS, 0.5, ALU.add, ALU.mult))
            st.link(v.tensor_scalar(y.bitcast(I32), half.bitcast(I32), -0.5, MAGIC_MINUS, ALU.mult, ALU.add))
            for _ in range(3):
                st.link(v.tensor_scalar(t1, y, y, half, ALU.mult, ALU.mult))
                st.link(v.scalar_tensor_tensor(y, t1, 1.5, y, ALU.subtract, ALU.mult))
            return y

        def bn_row(st, data, o):
            st.link(nc.vector.bn_stats(bn[:], data))
            st.eng.sem_inc(s_stats, 1)
            st.link(nc.vector.bn_aggr(sm[:, o:o + 2], bn[:]))

        def bn_chain(st, o):
            y = rsqrt_steps(st, sm[:, o + 1:o + 2], o + 2)
            st.link(nc.vector.scalar_tensor_tensor(sm[:, o + 5:o + 6], sm[:, o:o + 1], -1.0, y, ALU.mult, ALU.mult))
            return sm[:, o:o + 1], y, sm[:, o + 5:o + 6]

        def bn_steps(st, data, o):
            bn_row(st, data, o)
            return bn_chain(st, o)

        BN = 2 + 8 + 1

        def project_stage():
            s_x = [sem("x_loaded_even"), sem("x_loaded_odd")]
            s_st = [sem("h_stored_even"), sem("h_stored_odd")]
            s_v, s_xn, s_tp, s_tc, s_mm, s_ho = (sem(n) for n in (
                "proj_vector_steps", "xn_made", "xn_transposed", "xT_copied", "h_made", "h_copied"))
            xin = [sbs(f"xin{i}", [P, D]) for i in range(2)]
            xn = [sbs(f"xn{i}", [P, D]) for i in range(2)]
            xTs = [sbs(f"xTp{i}", [P, KT, P]) for i in range(2)]
            ho = [sbs(f"ho{i}", [P, RW]) for i in range(2)]
            KV = BN + 2
            HALF = (NT - 1) // 2

            with nc.Block() as block:
                @block.sync
                def _(sp):
                    def load(i, k, n=P):
                        sp.dma_start(xin[k][0:n, :], tile_rows(x, 2 * i + k, n)).then_inc(s_x[k], 16)

                    def store(i, k, n=P):
                        sp.wait_ge(s_ho, 2 * i + k + 1)
                        sp.dma_start(tile_rows(h_tab[0], 2 * i + k, n), ho[k][0:n, :]).then_inc(s_st[k], 16)
                    load(0, 0)
                    load(0, 1)
                    with sp.Fori(0, HALF - 1) as i:
                        for k in range(2):
                            sp.wait_ge(s_xn, 2 * i + k + 1)
                            load(i + 1, k)
                            store(i, k)
                    sp.wait_ge(s_xn, NT - 2)
                    load(HALF, 0, LAST)
                    store(HALF - 1, 0)
                    store(HALF - 1, 1)
                    store(HALF, 0, LAST)
                    sp.wait_ge(s_st[0], 16 * (HALF + 1))
                    sp.wait_ge(s_st[1], 16 * HALF)

                @block.vector
                def _(dve):
                    v = nc.vector

                    def body(i, k):
                        t = 2 * i + k
                        st = Steps(dve, s_v, KV * t)
                        dve.wait_ge(s_x[k], 16 * (i + 1))
                        mean, rstd, shift = bn_steps(st, xin[k][:], 0)
                        st.link(v.tensor_copy(stats[:, bass.ds(t, 1), 0:1], shift))
                        st.link(v.tensor_copy(stats[:, bass.ds(t, 1), 1:2], rstd))
                        assert st.n == KV
                        need(dve, s_tp, t - 1)
                        v.tensor_scalar(xn[k][:], xin[k][:], mean, rstd, ALU.subtract, ALU.mult).then_inc(s_xn, 1)
                    body(0, 0)
                    body(0, 1)
                    with dve.Fori(1, HALF) as i:
                        body(i, 0)
                        body(i, 1)
                    body(HALF, 0)

                @block.tensor
                def _(pe):
                    m = nc.tensor

                    def turn(t, k):
                        pe.wait_ge(s_xn, t + 1)
                        need(pe, s_tc, t)
                        for j in range(KT):
                            ins = m.transpose(tr_ps[:, j * P:(j + 1) * P], xn[k][:, j * P:(j + 1) * P], ident[:])
                        ins.then_inc(s_tp, 1)

                    def project(t, k):
                        pe.wait_ge(s_tc, t + 1)
                        need(pe, s_ho, t - 1)
                        bank, small = (dense_ps, small_ps) if k == 0 else (hid0_ps, hid1_ps)
                        for j in range(KT):
                            m.matmul(bank[:], xTs[k][:, j, :], Wc[0][:, j, :], start=(j == 0), stop=(j == KT - 1))
                        for j in range(KT):
                            ins = m.matmul(small[:, 0:16], xTs[k][:, j, :], WA[0][:, j, :], start=(j == 0), stop=(j == KT - 1))
                        ins.then_inc(s_mm, 1)

                    def both(i):
                        turn(2 * i + 1, 1)
                        project(2 * i, 0)
                        turn(2 * i + 2, 0)
                        project(2 * i + 1, 1)
                    turn(0, 0)
                    both(0)
                    with pe.Fori(1, HALF) as i:
                        both(i)
                    project(NT - 1, 0)

                @block.scalar
                def _(act):
                    a = nc.scalar

                    def copy_t(t, k):
                        act.wait_ge(s_tp, t + 1)
                        need(act, s_mm, t - 1)
                        a.copy(xTs[k][:], tr_ps[:].rearrange("p (k n) -> p k n", k=KT)).then_inc(s_tc, 1)

                    def copy_h(i, k):
                        t = 2 * i + k
                        bank, small = (dense_ps, small_ps) if k == 0 else (hid0_ps, hid1_ps)
                        act.wait_ge(s_mm, t + 1)
                        need(act, s_st[k], 16 * i)
                        a.copy(ho[k][:, 0:D], bank[:])
                        a.copy(ho[k][:, D:D + 8], small[:, 0:8])
                        a.copy(AS[:, bass.ds(t, 1), :], small[:, 0:8].rearrange("p (a h) -> p a h", a=1))
                        a.copy(AD[:, bass.ds(t, 1), :], small[:, 8:16].rearrange("p (a h) -> p a h", a=1)).then_inc(s_ho, 1)

                    def both(i):
                        copy_t(2 * i + 1, 1)
                        copy_h(i, 0)
                        copy_t(2 * i + 2, 0)
                        copy_h(i, 1)
                    copy_t(0, 0)
                    both(0)
                    with act.Fori(1, HALF) as i:
                        both(i)
                    copy_h(HALF, 0)

        def reference_stage(c, nh):
            s_r, s_m, s_p, s_z, s_e = (sem(f"{w}{c + 1}") for w in (
                "ref_steps", "partition_max_made", "max_made", "own_logits_made", "own_weights_made"))
            u, r, q, w = (sbs(f"ref{i}_{c}", [P, NT, 8]) for i in range(4))
            with nc.Block() as block:
                @block.vector
                def _(dve):
                    st, v = Steps(dve, s_r), nc.vector
                    v.tensor_reduce(amaxp[:, 0:nh], AS[:, :, 0:nh].rearrange("p t h -> p h t"), AX.X, ALU.max).then_inc(s_m, 1)
                    dve.wait_ge(s_p, 1)
                    mb = amax[:, 0:nh].rearrange("p (a h) -> p a h", a=1).to_broadcast([P, NT, nh])
                    H_ = slice(0, nh)
                    st.link(v.tensor_tensor(u[:, :, H_], AD[:, :, H_], mb, ALU.add))
                    st.link(v.scalar_tensor_tensor(r[:, :, H_], u[:, :, H_], SLOPE, u[:, :, H_], ALU.mult, ALU.max))
                    for o, val in ((0, AD), (nh, r)):
                        st.link(v.tensor_copy(NRb[:, :, 0, o:o + nh], val[:, :, H_]))
                        st.link(v.tensor_tensor(q[:, :, H_], val[:, :, H_], NRb[:, :, 0, o:o + nh], ALU.subtract))
                        st.link(v.tensor_copy(NRb[:, :, 1, o:o + nh], q[:, :, H_]))
                        st.link(v.tensor_tensor(NRb[:, :, 2, o:o + nh], q[:, :, H_], NRb[:, :, 1, o:o + nh], ALU.subtract))
                    st.link(v.tensor_tensor(u[:, :, H_], AS[:, :, H_], AD[:, :, H_], ALU.add))
                    st.link(v.scalar_tensor_tensor(q[:, :, H_], u[:, :, H_], SLOPE, u[:, :, H_], ALU.mult, ALU.max))
                    st.link(v.tensor_tensor(w[:, :, H_], q[:, :, H_], r[:, :, H_], ALU.subtract))
                    v.tensor_scalar(u[:, :, H_], w[:, :, H_], 0.0, None, ALU.min).then_inc(s_z, 1)

                @block.scalar
                def _(act):
                    act.wait_ge(s_z, 1)
                    nc.scalar.activation(ES[:, :, 0:nh], u[:, :, 0:nh], ACT.Exp).then_inc(s_e, 1)
                    act.wait_ge(s_e, 1)

                @block.gpsimd
                def _(pool):
                    pool.wait_ge(s_m, 1)
                    nc.gpsimd.partition_all_reduce(amax[:, 0:nh], amaxp[:, 0:nh], P, bass.bass_isa.ReduceOp.max).then_inc(s_p, 1)

        def conv_stage(c, nh):
            first = c == 0
            n = lambda w: f"{w}{c + 1}"
            s_row = [sem(n(f"rows_of_{w}_quads")) for w in ("even", "odd")]
            s_rb = [sem(n(f"rel_landed_slot{k}_")) for k in range(2)]
            (s_rows, s_rel, s_ST, s_adE, s_z, s_e, s_S, s_sq, s_msg, s_main, s_evac, s_idx, s_taken,
             s_pv) = (sem(n(w)) for w in (
                 "rows_landed", "rel_landed", "onehotT_made", "node_values_made", "logits_made", "weights_made",
                 "onehot_made", "squares_made", "messages_made", "visits_done", "acc_copied", "indices_copied",
                 "slots_taken", "quad_vector_steps"))
            s_acc = [sem(n("acc_stored_even")), sem(n("acc_stored_odd"))]
            rows = sbs(n("rows"), [P, RING, RW])
            relB = sbs(n("relB"), [P, 2, 4 * P], BF16)
            idx = sbs(n("idx"), [P, RING], I32)
            ST = sbs(n("ST"), [P, 4, P], BF16)
            S = [sbs(n(f"S{k}_"), [P, P]) for k in range(4)]
            sq = sbs(n("sq"), [P, 4, P]) if first else None
            msg = [sbs(n(f"msg{k}_"), [P, D]) for k in range(4)] if first else None
            z1, z2, z3, z4 = (sbs(n(f"z{k}_"), [P, 4, 8]) for k in range(4))
            e_s = sbs(n("e_s"), [P, 2, 4, 8])
            accS = [sbs(n(f"accS{k}_"), [P, RW]) for k in range(2)]
            acc_ps2, den_ps2 = (acc_ps, tr_ps), (small_ps, dense_ps)
            HALF = (NT - 1) // 2

            def bounds(eng, t):
                a = eng.value_load(q_end[0:1, bass.ds(t, 1)], min_val=0, max_val=QMAX)
                b = eng.value_load(q_end[0:1, bass.ds(t + 1, 1)], min_val=1, max_val=QMAX)
                return a, b

            def tiles(eng, tile):
                for t in range(4):
                    tile(t // 2, t % 2)
                with eng.Fori(2, HALF) as i:
                    tile(i, 0)
                    tile(i, 1)
                tile(HALF, 0)

            def heads(ap):
                return ap.rearrange("p (h c) -> p h c", h=nh)

            def spread(ap):
                return ap.rearrange("p (h a) -> p h a", a=1).to_broadcast([P, nh, D // nh])

            with nc.Block() as block:
                @block.gpsimd
                def _(pool):
                    turns = pool.value_load(q_end[0:1, NT + 1:NT + 2], min_val=2, max_val=QMAX // 4)
                    used = s_msg if first else s_main

                    def landed(i, q):
                        pool.wait_ge(s_row[q % 2], 64 * (2 * i + q // 2 + 1))
                        pool.sem_inc(s_rows, 1)

                    def turn(i):
                        for q in range(4):
                            nc.gpsimd.tensor_copy(idx[:, 4 * q:4 * q + 4], srcT[:, bass.ds(RING * i + 4 * q, 4)]).then_inc(s_idx, 1)
                            pool.wait_ge(s_idx, 4 * i + q + 1)
                            pool.wait_ge(used, RING * i + 4 * q + 4)
                            pool.sem_inc(s_taken, 1)
                            for k in range(4 * q, 4 * q + 4):
                                nc.gpsimd.indirect_dma_start(
                                    rows[:, k, :], None, h_tab[c],
                                    bass.IndirectOffsetOnAxis(ap=idx[:, k:k + 1], axis=0)).then_inc(s_row[q % 2], 16)
                            if q or not isinstance(i, int):
                                landed(i, q - 1)
                    turn(0)
                    with pool.Fori(1, turns) as i:
                        turn(i)
                    landed(turns, -1)

                @block.sync
                def _(sp):
                    pairs = 2 * sp.value_load(q_end[0:1, NT + 1:NT + 2], min_val=2, max_val=QMAX // 4)

                    def pair(i):
                        for k in range(2):
                            need(sp, s_ST, 2 * i + k - 1)
                            sp.dma_start(relB[:, k, :], rel_tab[bass.ds(8 * i + 4 * k, 4), :].rearrange("(a v) e -> a (v e)", a=1).to_broadcast([P, 4 * P])).then_inc(s_rb[k], 16)
                            if k or not isinstance(i, int):
                                sp.wait_ge(s_rb[1 - k], 16 * i + (16 if k else 0))
                                sp.sem_inc(s_rel, 1)
                    pair(0)
                    with sp.Fori(1, pairs + 1) as i:
                        pair(i)
                    sp.wait_ge(s_rb[1], 16 * pairs + 16)
                    sp.sem_inc(s_rel, 1)

                @block.vector
                def _(dve):
                    v = nc.vector
                    KQ = 3

                    def front(u):
                        dve.wait_ge(s_rel, u + 1)
                        need(dve, s_adE, u)
                        v.tensor_scalar(ST[:].rearrange("p v e -> p (v e)"), relB[:, bass.ds(u % 2, 1), :].rearrange("p a k -> p (a k)"), iota_p[:], None, ALU.is_equal).then_inc(s_ST, 1)

                    def quad(u):
                        st = Steps(dve, s_pv, KQ * u)
                        slot = (u % 4) * 4
                        adE = nodes_ps[:, 0:64].rearrange("p (v k) -> p v k", v=4)
                        dve.wait_ge(s_adE, u + 1)
                        dve.wait_ge(s_rows, u + 1)
                        st.link(v.tensor_tensor(z1[:, :, 0:nh], rows[:, bass.ds(slot, 4), D:D + nh], adE[:, :, 0:nh], ALU.add))
                        st.link(v.scalar_tensor_tensor(z2[:, :, 0:nh], z1[:, :, 0:nh], SLOPE, z1[:, :, 0:nh], ALU.mult, ALU.max))
                        st.link(v.tensor_tensor(z3[:, :, 0:nh], z2[:, :, 0:nh], adE[:, :, nh:2 * nh], ALU.subtract))
                        assert st.n == KQ
                        v.tensor_scalar(z4[:, :, 0:nh], z3[:, :, 0:nh], 0.0, None, ALU.min).then_inc(s_z, 1)
                        front(u + 1)
                        dve.wait_ge(s_e, u + 1)
                        for k in range(4):
                            dve.wait_ge(s_main, 4 * u + k + 1 + RING - 4)
                            e_k = e_s[:, bass.ds(u % 2, 1), k, 0:nh].rearrange("p a h -> p (a h)")
                            if first:
                                v.tensor_tensor(heads(msg[k][:]), heads(rows[:, bass.ds(slot + k, 1), 0:D].rearrange("p a n -> p (a n)")),
                                                spread(e_k), ALU.mult).then_inc(s_msg, 1)
                            else:
                                v.tensor_scalar(S[k][:], iota_n[:], relN[:, bass.ds(4 * u + k, 1)], e_k, ALU.is_equal, ALU.mult).then_inc(s_msg, 1)

                    if first:
                        dve.sem_inc(s_msg, RING)
                    front(0)

                    def tile(i, k):
                        a, b = bounds(dve, 2 * i + k)
                        with dve.Fori(a, b) as u:
                            quad(u)
                    tiles(dve, tile)

                @block.scalar
                def _(act):
                    a_ = nc.scalar

                    def squares(u):
                        need(act, s_S, 4 * u)
                        for k in range(4):
                            a_.activation(sq[:, k, :], iota_n[:], ACT.Square, bias=relN[:, bass.ds(4 * u + k, 1)], scale=-1.0).then_inc(s_sq, 1)

                    def quad(u):
                        act.wait_ge(s_z, u + 1)
                        act.wait_ge(s_main, 4 * u - 4 + RING)
                        a_.activation(e_s[:, bass.ds(u % 2, 1), :, 0:nh].rearrange("p a v h -> p (a v) h"), z4[:, :, 0:nh], ACT.Exp).then_inc(s_e, 1)
                        if first:
                            act.wait_ge(s_sq, 4 * u + 4)
                            for k in range(4):
                                act.wait_ge(s_main, 4 * u + k + 1 + RING - 4)
                                a_.activation(S[k][:], sq[:, k, :], ACT.Relu, bias=ones[:, 0:1], scale=-1.0).then_inc(s_S, 1)
                            squares(u + 1)

                    def evacuate(i, k):
                        t = 2 * i + k
                        act.wait_ge(s_main, act_end[k] * 4 + RING)
                        need(act, s_acc[k], 16 * i)
                        a_.copy(accS[k][:, 0:D], acc_ps2[k][:]).then_inc(s_evac, 1)
                        a_.copy(accS[k][:, D:RW], den_ps2[k][:, 0:8]).then_inc(s_evac, 1)
                        act.wait_ge(s_evac, 2 * t + 2)
                        act.dma_start(tile_rows(acc_tab, t), accS[k][:]).then_inc(s_acc[k], 16)

                    act_end = [None, None]

                    def tile(i, k):
                        a, b = bounds(act, 2 * i + k)
                        with act.Fori(a, b) as u:
                            quad(u)
                        act_end[1 - k] = a
                        if k:
                            evacuate(i, 0)
                        elif not (isinstance(i, int) and i == 0):
                            evacuate(i - 1, 1)
                        act_end[k] = b
                    if first:
                        squares(0)
                    tiles(act, tile)
                    evacuate(HALF, 0)
                    act.wait_ge(s_acc[0], 16 * (HALF + 1))
                    act.wait_ge(s_acc[1], 16 * HALF)

                @block.tensor
                def _(pe):
                    m = nc.tensor
                    pe.sem_inc(s_main, RING)

                    def front(u):
                        tq = pe.value_load(quad_tile[0:1, bass.ds(u, 1)], min_val=0, max_val=NT - 1)
                        pe.wait_ge(s_ST, u + 1)
                        for k in range(4):
                            for part in range(3):
                                ins = m.matmul(nodes_ps[:, 16 * k:16 * k + 2 * nh], ST[:, k, :], NRb[:, bass.ds(tq, 1), part, 0:2 * nh].rearrange("p a k -> p (a k)"),
                                               start=(part == 0), stop=(part == 2), skip_group_check=True)
                        ins.then_inc(s_adE, 1)

                    def quad(u, bank, den_bank):
                        front(u + 1)
                        for k in range(4):
                            pe.wait_ge(s_msg, 4 * u + k + 1 + (RING if first else 0))
                            if first:
                                pe.wait_ge(s_S, 4 * u + k + 1)
                            rhs = msg[k][:] if first else rows[:, bass.ds((u % 4) * 4 + k, 1), 0:D].rearrange("p a n -> p (a n)")
                            den = e_s[:, bass.ds(u % 2, 1), k, 0:nh].rearrange("p a h -> p (a h)") if first else ones[:, 0:2]
                            m.matmul(den_bank[:, 0:max(nh, 2)], S[k][:], den, start=False, stop=False, skip_group_check=True)
                            m.matmul(bank[:], S[k][:], rhs, start=False, stop=False, skip_group_check=True).then_inc(s_main, 1)

                    front(0)

                    def tile(i, k):
                        a, b = bounds(pe, 2 * i + k)
                        need(pe, s_evac, 2 * (2 * i + k - 1))
                        m.matmul(acc_ps2[k][:], zero_b[:, 0:P], zero_b[:], start=True, stop=False, skip_group_check=True)
                        m.matmul(den_ps2[k][:, 0:16], zero_b[:, 0:P], zero_b[:, 0:16], start=True, stop=False, skip_group_check=True)
                        with pe.Fori(a, b) as u:
                            quad(u, acc_ps2[k], den_ps2[k])
                    tiles(pe, tile)

        def node_stage(c, nh):
            first = c == 0
            bias, gain, shift = (vecs[:, 3 * c + i, :] for i in range(3))
            n = lambda w: f"{w}{c + 1}"
            first_only = ("node_h_made", "node_h_copied")
            second_only = ("residual_summed", "x_normed", "gate_made", "combine_made", "combine_transposed", "combine_copied",
                           "hidden_relu", "weights_spread", "hidden_weighted", "ffn_made", "out_made", "x2_stats_made")
            (s_v, s_nn, s_norm, s_y, s_el, s_mid, s_xl, s_tp, s_tc, s_mm, s_ho, s_g, s_gz, s_ge, s_cw, s_ct,
             s_ctc, s_hid, s_relu, s_crep, s_hs, s_fo, s_out, s_x2n, s_hs0,
             s_own, s_sum, s_pl) = (None if w in (second_only if first else first_only) else sem(n(w)) for w in (
                 "node_vector_steps", "node_stats_made", "normed", "affine_made", "elu_parts_made", "x_new_made",
                 "x_normed", "x_transposed", "node_xT_copied", "node_h_made", "node_h_copied", "gate_made",
                 "gate_shifted", "gate_exp_made", "combine_made", "combine_transposed", "combine_copied",
                 "hidden_made", "hidden_relu", "weights_spread", "hidden_weighted", "ffn_made", "out_made",
                 "x2_stats_made", "xn_or_relu_made", "own_loop_made", "residual_summed", "pool_steps"))
            s_in = [sem(n("node_inputs_even")), sem(n("node_inputs_odd"))]
            s_res = [sem(n("residual_even")), sem(n("residual_odd"))]
            s_sa = [sem(n("node_store_even")), sem(n("node_store_odd"))]
            s_sb = [sem(n("node_h_store_even")), sem(n("node_h_store_odd"))] if first else None
            two = lambda name, w: [sbs(n(f"{name}{k}_"), [P, w]) for k in range(2)]
            ac, ht, xt = two("ac", RW), two("ht", RW), two("xt", D)
            x1t = None if first else two("x1t", D)
            B1, B2 = two("B1", D), two("B2", D)
            NM, Y, RP, EX, XN = two("NM", D), two("Y", D), two("RP", D), two("EX", D), two("XN", D)
            X1 = two("X1", D)
            smn = [sbs(n(f"smn{k}_"), [P, 2]) for k in range(2)]
            sm2 = [sbs(n(f"sm2{k}_"), [P, 2]) for k in range(2)]
            xT = [sbs(n(f"nxT{k}_"), [P, KT, P]) for k in range(2)]
            ho = two("nho", RW) if first else None
            if not first:
                XL = sbs(n("XL"), [P, D])
                hs = sbs(n("hs"), [P, 2, 4, P])
                cw = [sbs(n(f"cw{k}_"), [P, 16]) for k in range(2)]
                ctr = [sbs(n(f"ctr{k}_"), [NE + 1, P]) for k in range(2)]
                c3 = [sbs(n(f"cmp{i}_"), [P, NE, NE]) for i in range(3)]
                g8 = sbs(n("g8"), [P, 8, 8])
                OUT = two("OUT", D)
            small8 = sbs(n("den8"), [P, 2, 8])
            LAGS = 1 if first else 2
            HALF = (NT - 1) // 2

            def steps(eng, step):
                for s in range(4):
                    step(s // 2, s % 2)
                with eng.Fori(2, HALF - 1) as i:
                    step(i, 0)
                    step(i, 1)
                for s in range(NT - 3, NT + LAGS):
                    step(s // 2, s % 2)

            def at(i, k, back):
                if isinstance(i, int):
                    s = 2 * i + k - back
                    return (s, s // 2, s % 2) if 0 <= s < NT else None
                return (2 * i + k - back, i - (back - k + 1) // 2, (k - back) % 2)

            def heads(ap):
                return ap.rearrange("p (h c) -> p h c", h=nh)

            def spread(ap):
                return ap.rearrange("p (h a) -> p h a", a=1).to_broadcast([P, nh, D // nh])

            def size(t):
                return LAST if isinstance(t, int) and t == NT - 1 else P

            with nc.Block() as block:
                @block.sync
                def _(sp):
                    def load_sums(t, i, k):
                        r = size(t)
                        need(sp, s_nn, t - 1)
                        sp.dma_start(ac[k][:], tile_rows(acc_tab, t)).then_inc(s_in[k], 16)
                        sp.dma_start(ht[k][0:r, :], tile_rows(h_tab[c], t, r)).then_inc(s_in[k], 16)

                    def load_residual(t, i, k):
                        r = size(t)
                        need(sp, s_mid, t - 1)
                        sp.dma_start(xt[k][0:r, :], tile_rows(x, t, r)).then_inc(s_res[k], 16)
                        if not first:
                            sp.dma_start(x1t[k][0:r, :], tile_rows(x1_tab, t, r)).then_inc(s_res[k], 16)

                    def step(i, k):
                        if it := at(i, k, -1):
                            load_sums(*it)
                            load_residual(*it)
                        if it := at(i, k, LAGS):
                            t, j, kk = it
                            r = size(t)
                            if first:
                                sp.wait_ge(s_mid, t + 1)
                                sp.dma_start(tile_rows(x1_tab, t, r), X1[kk][0:r, :]).then_inc(s_sa[kk], 16)
                                sp.wait_ge(s_ho, t + 1)
                                sp.dma_start(tile_rows(h_tab[1], t, r), ho[kk][0:r, :]).then_inc(s_sb[kk], 16)
                            else:
                                sp.wait_ge(s_out, t + 1)
                                sp.dma_start(tile_rows(out, t, r), OUT[kk][0:r, :]).then_inc(s_sa[kk], 16)
                    load_sums(0, 0, 0)
                    load_residual(0, 0, 0)
                    steps(sp, step)
                    for q in (s_sa, s_sb) if first else (s_sa,):
                        sp.wait_ge(q[0], 16 * (HALF + 1))
                        sp.wait_ge(q[1], 16 * HALF)

                @block.gpsimd
                def _(pool):
                    g_ = nc.gpsimd

                    def own_loop(t, j, k):
                        pool.wait_ge(s_in[k], 32 * (j + 1))
                        need(pool, s_nn, t - 1)
                        own = ES[:, bass.ds(t, 1), 0:nh].rearrange("p a h -> p (a h)")
                        g_.tensor_tensor(heads(B1[k][:]), heads(ht[k][:, 0:D]), spread(own), ALU.mult).then_inc(s_own, 1)

                    def affine(t, j, k):
                        pool.wait_ge(s_norm, t + 1)
                        g_.tensor_tensor(NM[k][:], NM[k][:], gain, ALU.mult).then_inc(s_pl, 1)
                        pool.wait_ge(s_pl, t + 1)
                        g_.tensor_tensor(Y[k][:], NM[k][:], shift, ALU.add).then_inc(s_y, 1)

                    def residual(t, j, k):
                        pool.wait_ge(s_res[k], 32 * (j + 1))
                        g_.tensor_tensor(xt[k][:], xt[k][:], x1t[k][:], ALU.add).then_inc(s_sum, 1)

                    def step(i, k):
                        if it := at(i, k, -1):
                            own_loop(*it)
                        if it := at(i, k, 0):
                            if not first:
                                residual(*it)
                            affine(*it)
                    own_loop(0, 0, 0)
                    steps(pool, step)

                NS = 5 + BN if nh == 1 else 6 + BN
                K_NEW = NS
                K_AFTER = 1 if first else 1 + BN
                K_GATE = 0 if first else 15
                KS = K_NEW + K_AFTER + K_GATE

                @block.vector
                def _(dve):
                    v = nc.vector

                    def new(st, t, j, k):
                        dve.wait_ge(s_in[k], 32 * (j + 1))
                        own = ES[:, bass.ds(t, 1), 0:nh].rearrange("p a h -> p (a h)")
                        st.link(v.tensor_tensor(small8[:, 0, 0:nh], own, ac[k][:, D:D + nh], ALU.add))
                        st.link(v.reciprocal(small8[:, 1, 0:nh], small8[:, 0, 0:nh]))
                        dve.wait_ge(s_own, t + 1)
                        st.link(v.tensor_tensor(B2[k][:], B1[k][:], ac[k][:, 0:D], ALU.add))
                        if nh == 1:
                            st.link(v.scalar_tensor_tensor(B2[k][:], B2[k][:], small8[:, 1, 0:1], bias, ALU.mult, ALU.add))
                        else:
                            st.link(v.tensor_tensor(heads(B2[k][:]), heads(B2[k][:]), spread(small8[:, 1, 0:nh]), ALU.mult))
                            st.link(v.tensor_tensor(B2[k][:], B2[k][:], bias, ALU.add))
                        mean, rstd, sh = bn_steps(st, B2[k][:], 0)
                        st.link(v.tensor_copy(smn[k][:, 0:1], rstd))
                        v.tensor_copy(smn[k][:, 1:2], sh).then_inc(s_nn, 1)

                    def after(st, t, j, k):
                        dve.wait_ge(s_el, t + 1)
                        st.link(v.scalar_tensor_tensor(NM[k][:], EX[k][:], -1.0, RP[k][:], ALU.add, ALU.add))
                        if first:
                            need(dve, s_sa[k], 16 * j)
                            v.tensor_tensor(X1[k][:], NM[k][:], XN[k][:], ALU.add).then_inc(s_mid, 1)
                            return
                        need(dve, s_out, t - 1)
                        dve.wait_ge(s_sum, t + 1)
                        v.tensor_tensor(X1[k][:], NM[k][:], xt[k][:], ALU.add).then_inc(s_mid, 1)
                        dve.wait_ge(s_mid, t + 1)
                        mean, rstd, sh = bn_steps(st, X1[k][:], 8)
                        v.tensor_copy(sm2[k][:, 0:1], rstd).then_inc(s_x2n, 1)
                        v.tensor_copy(sm2[k][:, 1:2], sh).then_inc(s_x2n, 1)

                    def gate(st, t, j, k):
                        dve.wait_ge(s_g, t + 1)
                        g = crep_ps[:, 0:NE]
                        st.link(v.tensor_reduce(sm[:, 16:17], g, AX.X, ALU.max))
                        v.tensor_scalar(g8[:, 0, :], g, sm[:, 16:17], None, ALU.subtract).then_inc(s_gz, 1)
                        dve.wait_ge(s_ge, t + 1)
                        st.link(v.tensor_reduce(sm[:, 17:18], g8[:, 1, :], AX.X, ALU.add))
                        st.link(v.reciprocal(sm[:, 18:19], sm[:, 17:18]))
                        st.link(v.tensor_scalar(g8[:, 2, :], g8[:, 1, :], sm[:, 18:19], None, ALU.mult))
                        sj = g8[:, 2:3, :].to_broadcast([P, NE, NE])
                        se = g8[:, 2, :].rearrange("p (e a) -> p e a", a=1).to_broadcast([P, NE, NE])
                        st.link(v.tensor_tensor(c3[0][:], sj, se, ALU.is_gt))
                        st.link(v.tensor_tensor(c3[1][:], sj, se, ALU.is_equal))
                        st.link(v.tensor_tensor(c3[2][:], c3[1][:], less[:], ALU.mult))
                        st.link(v.tensor_tensor(c3[1][:], c3[2][:], c3[0][:], ALU.add))
                        st.link(v.tensor_reduce(g8[:, 3, :], c3[1][:], AX.X, ALU.add))
                        st.link(v.tensor_scalar(g8[:, 4, :], g8[:, 3, :], 1.5, None, ALU.is_lt))
                        st.link(v.tensor_tensor(g8[:, 5, :], g8[:, 4, :], g8[:, 2, :], ALU.mult))
                        st.link(v.tensor_reduce(sm[:, 19:20], g8[:, 5, :], AX.X, ALU.add))
                        st.link(v.tensor_scalar(sm[:, 20:21], sm[:, 19:20], 1e-20, None, ALU.add))
                        st.link(v.reciprocal(sm[:, 21:22], sm[:, 20:21]))
                        need(dve, s_ct, t - 1)
                        st.link(v.memset(cw[k][:, NE:NE + 1], 1.0))
                        v.tensor_scalar(cw[k][:, 0:NE], g8[:, 5, :], sm[:, 21:22], None, ALU.mult).then_inc(s_cw, 1)

                    def weigh(t, g):
                        dve.wait_ge(s_relu, FG * t + g + 1)
                        dve.wait_ge(s_crep, (FG - 1) * t + g)
                        hv = hs[:, g % 2].rearrange("p j n -> p (j n)")
                        v.tensor_tensor(hv, hv, crep_ps[:], ALU.mult).then_inc(s_hs, 1)

                    def output(t, j, k):
                        dve.wait_ge(s_fo, t + 1)
                        need(dve, s_sa[k], 16 * j)
                        v.tensor_tensor(OUT[k][:], X1[k][:], dense_ps[:], ALU.add).then_inc(s_out, 1)

                    def step(i, k):
                        st = Steps(dve, s_v, (count[0] if isinstance(i, int) else KS * (2 * i + k - 4) + count[1]))
                        before, mid, late = at(i, k, 0), at(i, k, 1), None if first else at(i, k, 2)
                        if late:
                            weigh(late[0], 1)
                        if mid:
                            after(st, *mid)
                        if late:
                            weigh(late[0], 2)
                        if before:
                            new(st, *before)
                        if late:
                            output(*late)
                        if mid and not first:
                            gate(st, *mid)
                        if isinstance(i, int):
                            count[0] += st.n
                            if (i, k) == (1, 1):
                                count[1] = count[0]
                                count[0] += KS * (NT - 7)
                        else:
                            assert st.n == KS, (st.n, KS)
                    count = [0, 0]
                    steps(dve, step)

                @block.scalar
                def _(act):
                    a_ = nc.scalar

                    def norm(t, j, k):
                        act.wait_ge(s_nn, t + 1)
                        a_.activation(NM[k][:], B2[k][:], ACT.Identity, bias=smn[k][:, 1:2], scale=smn[k][:, 0:1]).then_inc(s_norm, 1)
                        if first:
                            act.wait_ge(s_res[k], 16 * (j + 1))
                            sv = stats[:, bass.ds(t, 1), :].rearrange("p a k -> p (a k)")
                            a_.activation(XN[k][:], xt[k][:], ACT.Identity, bias=sv[:, 0:1], scale=sv[:, 1:2]).then_inc(s_hs0, 1)

                    def elu(t, j, k):
                        act.wait_ge(s_y, t + 1)
                        a_.activation(RP[k][:], Y[k][:], ACT.Relu).then_inc(s_gz if first else s_hs0, 1)
                        a_.activation(B2[k][:], Y[k][:], ACT.Relu, scale=-1.0).then_inc(s_ge if first else s_ct0, 1)
                        act.wait_ge(s_ge if first else s_ct0, t + 1)
                        a_.activation(EX[k][:], B2[k][:], ACT.Exp, scale=-1.0).then_inc(s_el, 1)

                    def copy_t(t, j, k):
                        act.wait_ge(s_tp, t + 1)
                        a_.copy(xT[k][:], tr_ps[:].rearrange("p (k n) -> p k n", k=KT)).then_inc(s_tc, 1)

                    def copy_h(t, j, k):
                        act.wait_ge(s_mm, t + 1)
                        need(act, s_sb[k], 16 * j)
                        a_.copy(ho[k][:, 0:D], dense_ps[:])
                        a_.copy(ho[k][:, D:D + 1], small_ps[:, 0:1])
                        a_.copy(AS[:, bass.ds(t, 1), 0:1].rearrange("p a h -> p (a h)"), small_ps[:, 0:1])
                        a_.copy(AD[:, bass.ds(t, 1), 0:1].rearrange("p a h -> p (a h)"), small_ps[:, 1:2]).then_inc(s_ho, 1)

                    def norm2(t, j, k):
                        act.wait_ge(s_x2n, 2 * t + 2)
                        need(act, s_tp, t)
                        a_.activation(XL[:], X1[k][:], ACT.Identity, bias=sm2[k][:, 1:2], scale=sm2[k][:, 0:1]).then_inc(s_xl, 1)

                    def relus(t, g):
                        act.wait_ge(s_hid, FG * t + g + 1)
                        if g < 2:
                            need(act, s_fo if g == 0 else s_hs1, t)
                        else:
                            act.wait_ge(s_h0u, t + 1)
                        for q in range(4):
                            ins = a_.activation(hs[:, g % 2, q, :], (hid0_ps, hid1_ps)[g % 2][:, q * P:(q + 1) * P], ACT.Relu, bias=hb[:, 4 * g + q:4 * g + q + 1])
                        ins.then_inc(s_relu, 1)

                    def step(i, k):
                        before, mid, late = at(i, k, 0), at(i, k, 1), at(i, k, 2)
                        if not first:
                            if late:
                                relus(late[0], 0)
                                relus(late[0], 1)
                                act.wait_ge(s_ct, late[0] + 1)
                                a_.copy(ctr[late[2]][:], small_ps[0:NE + 1, 0:P]).then_inc(s_ctc, 1)
                            if mid:
                                elu(*mid)
                            if late:
                                relus(late[0], 2)
                            if mid:
                                norm2(*mid)
                                copy_t(*mid)
                            if before:
                                norm(*before)
                            if mid:
                                act.wait_ge(s_gz, mid[0] + 1)
                                a_.activation(g8[:, 1, :], g8[:, 0, :], ACT.Exp).then_inc(s_ge, 1)
                            return
                        if before:
                            norm(*before)
                        if mid:
                            copy_t(*mid)
                        if before:
                            elu(*before)
                        if mid:
                            copy_h(*mid)
                    if first:
                        for k in range(2):
                            a_.copy(ho[k][:, D:RW], ones[:, 0:8]).then_inc(s_hid, 1)
                        act.wait_ge(s_hid, 2)
                    steps(act, step)

                @block.tensor
                def _(pe):
                    m = nc.tensor

                    def turn(t, k):
                        src_t = X1[k] if first else XL
                        pe.wait_ge(s_mid if first else s_xl, t + 1)
                        need(pe, s_tc, t)
                        for j in range(KT):
                            ins = m.transpose(tr_ps[:, j * P:(j + 1) * P], src_t[:, j * P:(j + 1) * P], ident[:])
                        ins.then_inc(s_tp, 1)

                    def layer2(t, k):
                        pe.wait_ge(s_tc, t + 1)
                        need(pe, s_ho, t)
                        for j in range(KT):
                            m.matmul(dense_ps[:], xT[k][:, j, :], Wc[1][:, j, :], start=(j == 0), stop=(j == KT - 1))
                        for j in range(KT):
                            ins = m.matmul(small_ps[:, 0:2], xT[k][:, j, :], WA[1][:, j, 0:2], start=(j == 0), stop=(j == KT - 1))
                        ins.then_inc(s_mm, 1)

                    def hidden(t, k, g):
                        need(pe, s_relu, FG * t + (0 if g == 0 else -1 if g == 1 else 1))
                        for j in range(4):
                            for q in range(KT):
                                w = sw1_s[:, q, j * P:(j + 1) * P] if g == 0 else w1_s[:, q, 4 * (g - 1) + j, :]
                                ins = m.matmul((hid0_ps, hid1_ps)[g % 2][:, j * P:(j + 1) * P], w, xT[k][:, q, :], start=(q == 0), stop=(q == KT - 1), skip_group_check=True)
                        ins.then_inc(s_hid, 1)

                    def spread_weights(t, k, g):
                        if g == 1:
                            pe.wait_ge(s_ctc, t + 1)
                        else:
                            pe.wait_ge(s_hs, (FG - 1) * t + 1)
                        for j in range(4):
                            ins = m.matmul(crep_ps[:, j * P:(j + 1) * P], sel[:, 4 * (g - 1) + j, :], ctr[k][:], start=True, stop=True, skip_group_check=True)
                        ins.then_inc(s_crep, 1)

                    def output(t, g):
                        if g == 0:
                            pe.wait_ge(s_relu, FG * t + 1)
                            need(pe, s_out, t)
                        else:
                            pe.wait_ge(s_hs, (FG - 1) * t + g)
                        for j in range(4):
                            w = sw2_s[:, j, :] if g == 0 else w2_s[:, 4 * (g - 1) + j, :]
                            ins = m.matmul(dense_ps[:], hs[:, g % 2, j, :], w, start=(g == 0 and j == 0), stop=(g == 2 and j == 3))
                        ins.then_inc((s_h0u, s_hs1, s_fo)[g], 1)

                    def step(i, k):
                        before, mid, late = at(i, k, 0), at(i, k, 1), at(i, k, 2)
                        if first:
                            if mid:
                                turn(mid[0], mid[2])
                                layer2(mid[0], mid[2])
                            return
                        if late:
                            t, kk = late[0], late[2]
                            hidden(t, kk, 0)
                            hidden(t, kk, 1)
                            pe.wait_ge(s_cw, t + 1)
                            need(pe, s_ctc, t)
                            m.transpose(small_ps[0:NE + 1, 0:P], cw[kk][:, 0:NE + 1], ident[:]).then_inc(s_ct, 1)
                            output(t, 0)
                            spread_weights(t, kk, 1)
                            m.matmul(dense_ps[:], ctr[kk][:], b2c[:], start=False, stop=False)
                            hidden(t, kk, 2)
                            output(t, 1)
                            spread_weights(t, kk, 2)
                        if mid:
                            turn(mid[0], mid[2])
                        if late:
                            output(t, 2)
                        if mid:
                            t2, k2 = mid[0], mid[2]
                            pe.wait_ge(s_tc, t2 + 1)
                            if late:
                                pe.wait_ge(s_hs, (FG - 1) * t + 2)
                            for j in range(KT):
                                ins = m.matmul(crep_ps[:, 0:NE], xT[k2][:, j, :], gateT[:, j, :], start=(j == 0), stop=(j == KT - 1))
                            ins.then_inc(s_g, 1)
                    steps(pe, step)

        s_stats, s_ct0, s_hs1, s_h0u = (sem(n) for n in ("row_stats_made", "minus_relu_made", "hidden1_used", "hidden0_used"))
        with ExitStack() as ctx_stage:
            setup_stage()
        stages = [(project_stage,), (reference_stage, 0, H), (conv_stage, 0, H), (node_stage, 0, H),
                  (reference_stage, 1, 1), (conv_stage, 1, 1), (node_stage, 1, 1)]
        for stage, *args in stages:
            with ExitStack() as ctx_stage:
                def sbs(name, shape, dt=F32):
                    return ctx_stage.enter_context(nc.sbuf_tensor(name, shape, dt))
                stage(*args)


_INS = ["x", "src", "dst"] + ["L0_gnn_" + n for n in ("W1", "a_src1", "a_dst1", "b1", "g1", "beta1", "W2", "a_src2", "a_dst2", "b2", "g2", "beta2")] \
    + ["L0_ffn_" + n for n in ("gate_w", "w1", "b1", "w2", "b2", "sw1", "sb1", "sw2", "sb2")]


def kernel(**inputs):
    import numpy as _np
    import concourse.bacc as _bacc
    from concourse import mybir as _mybir
    from concourse.bass_utils import run_bass_kernel_spmd as _run

    nc = _bacc.Bacc("TRN2", target_bir_lowering=False, num_devices=1)
    arrays, args = {}, []
    for name in _INS:
        a = _np.ascontiguousarray(inputs[name])
        arrays[f"in_{name}_dram"] = a
        args.append(nc.dram_tensor(f"in_{name}_dram", a.shape, _mybir.dt.from_np(a.dtype), kind="ExternalInput").ap())
    shape = tuple(inputs["x"].shape)
    args.append(nc.dram_tensor("out_0_dram", shape, _mybir.dt.float32, kind="ExternalOutput").ap())
    gnn_ffn(nc, *args)
    r = _run(nc, [arrays], core_ids=[0])
    return r.results[0]["out_0_dram"]
```

```python
from contextlib import ExitStack

import concourse.bass as bass
from concourse import mybir

ALU = mybir.AluOpType
ACT = mybir.ActivationFunctionType
AX = mybir.AxisListType
F32 = mybir.dt.float32
I32 = mybir.dt.int32
BF16 = mybir.dt.bfloat16

P = 128
D = 512
KT = D // P
EPS = 1e-5
SLOPE = 0.2
MAGIC_MINUS = float(0x5F3759DF - (1 << 31) - (1 << 22))
OUTSIDE = 30000.0
SPAN = 60.0


class Steps:

    def __init__(self, eng, sem, base=0):
        self.eng, self.sem, self.base, self.n = eng, sem, base, 0

    def link(self, ins):
        self.n += 1
        ins.then_inc(self.sem, 1)
        self.eng.wait_ge(self.sem, self.base + self.n)


def need(eng, sem, n):
    if not isinstance(n, int) or n > 0:
        eng.wait_ge(sem, n)


def gnn_ffn(nc, x, src, dst, W1, a_src1, a_dst1, b1, g1, beta1, W2, a_src2, a_dst2, b2, g2, beta2,
            gate_w, w1, fb1, w2, fb2, sw1, sb1, sw2, sb2, out):
    N = x.shape[0]
    E = src.shape[0]
    H = a_src1.shape[0]
    C = D // H
    NE = gate_w.shape[0]
    NT = -(-N // P)
    LAST = N - (NT - 1) * P
    CG = -(-(E + P) // (P * P))
    CH = P * CG
    NCH = -(-E // P)
    RING = 16
    QMAX = -(-(NCH + NT + 3 * NT) // RING) * 4
    VG = -(-4 * (QMAX + 2) // P)
    QG = -(-(QMAX + 2) // P)
    RW = D + 8
    FG = 3
    assert NT < 256 and int(OUTSIDE) // P >= NT
    assert NCH < CH and LAST > 0 and C * H == D and NE == 8

    with ExitStack() as ctx:
        def sb(name, shape, dt=F32):
            return ctx.enter_context(nc.sbuf_tensor(name, shape, dt))

        def sem(name):
            return ctx.enter_context(nc.semaphore(name))

        banks = [ctx.enter_context(nc.psum_tensor(f"bank{i}", [P, 512], F32)) for i in range(8)]
        acc_ps, nodes_ps, tr_ps, dense_ps, hid0_ps, hid1_ps, crep_ps, small_ps = banks

        edge_tab = nc.dram_tensor("edge_tab", (CH, 2 * P), F32).ap()
        rel_tab = nc.dram_tensor("rel_tab", (VG * P, P), BF16).ap()
        h_tab = [nc.dram_tensor(f"h_tab{i}", (N, RW), F32).ap() for i in (1, 2)]
        x1_tab = nc.dram_tensor("x1_tab", (N, D), F32).ap()

        acc_tab = nc.dram_tensor("acc_tab", (NT * P, RW), F32).ap()

        ident = sb("ident", [P, P])
        iota_n = sb("iota_n", [P, P])
        iota_p = sb("iota_p", [P, 1])
        ones = sb("ones", [P, P])
        zero_b = sb("zero_b", [P, 512], BF16)
        less = sb("less", [P, NE, NE])
        relN = sb("relN", [P, VG * P])
        srcT = sb("srcT", [P, VG * P], I32)
        quad_tile = sb("quad_tile", [1, QG * P], I32)
        q_end = sb("q_end", [P, NT + 2], I32)
        Wc = [sb("W1s", [P, KT, D]), sb("W2s", [P, KT, D])]
        WA = [sb("WA1", [P, KT, 16]), sb("WA2", [P, KT, 16])]
        vecs = sb("vecs", [P, 6, D])
        sw1_s = sb("sw1_s", [P, KT, D])
        w1_s = sb("w1_s", [P, KT, NE, P])
        sw2_s = sb("sw2_s", [P, KT, D])
        w2_s = sb("w2_s", [P, NE, D])
        gateT = sb("gateT", [P, KT, NE])
        hb = sb("hb", [P, 12])
        b2c = sb("b2c", [NE + 1, D])
        sel = sb("sel", [NE + 1, NE, P])
        AS = sb("AS", [P, NT, 8])
        AD = sb("AD", [P, NT, 8])
        NRb = sb("NRb", [P, NT, 3, 16], BF16)
        ES = sb("ES", [P, NT, 8])
        amax = sb("amax", [P, 16])
        amaxp = sb("amaxp", [P, 16])
        stats = sb("stats", [P, NT, 2])
        sm = sb("sm", [P, 32])
        bn = sb("bn", [P, 6])

        def tile_rows(tab, t, n=P):
            return tab[bass.ds(t * P, n), :] if n == P else tab[(NT - 1) * P:N, :]

        def setup_stage():
            dstage = ctx_stage.enter_context(nc.sbuf_tensor("dstage", [P, CG * P], I32))
            sstage = ctx_stage.enter_context(nc.sbuf_tensor("sstage", [P, CG * P], I32))
            et = ctx_stage.enter_context(nc.sbuf_tensor("et", [P, CG, 2 * P], F32))
            vt = ctx_stage.enter_context(nc.sbuf_tensor("vt", [P, VG, 2 * P], F32))
            cnt = ctx_stage.enter_context(nc.sbuf_tensor("cnt", [P, 64], F32))
            f = [ctx_stage.enter_context(nc.sbuf_tensor(f"f{i}", [P, 64], F32)) for i in range(8)]
            n_i = [ctx_stage.enter_context(nc.sbuf_tensor(f"n{i}", [P, 64], I32)) for i in range(4)]
            big = ctx_stage.enter_context(nc.sbuf_tensor("big", [P, VG, NT], F32))
            big2 = ctx_stage.enter_context(nc.sbuf_tensor("big2", [P, VG, NT], F32))
            big3 = ctx_stage.enter_context(nc.sbuf_tensor("big3", [P, QG, NT], F32))
            qt = ctx_stage.enter_context(nc.sbuf_tensor("qt", [P, QG], F32))
            qdiag = ctx_stage.enter_context(nc.sbuf_tensor("qdiag", [P, QG * P], F32))
            relb = ctx_stage.enter_context(nc.sbuf_tensor("relb", [P, VG, P], BF16))
            vnum = ctx_stage.enter_context(nc.sbuf_tensor("vnum", [P, VG], F32))
            vt_t = ctx_stage.enter_context(nc.sbuf_tensor("vt_t", [P, VG], F32))
            vt_c = ctx_stage.enter_context(nc.sbuf_tensor("vt_c", [P, VG], F32))
            vt_o = ctx_stage.enter_context(nc.sbuf_tensor("vt_o", [P, VG], F32))
            vt_ci = ctx_stage.enter_context(nc.sbuf_tensor("vt_ci", [P, VG], I32))
            junk = ctx_stage.enter_context(nc.sbuf_tensor("junk", [P, CG * P], BF16))
            dtile = ctx_stage.enter_context(nc.sbuf_tensor("dtile", [P, CG * P], I32))
            dtile_b = ctx_stage.enter_context(nc.sbuf_tensor("dtile_b", [P, CG * P], BF16))
            ab = ctx_stage.enter_context(nc.sbuf_tensor("ab", [P, 4, D], F32))
            gnat = ctx_stage.enter_context(nc.sbuf_tensor("gnat", [NE, D], F32))
            hbn = ctx_stage.enter_context(nc.sbuf_tensor("hbn", [12, P], F32))
            prod = ctx_stage.enter_context(nc.sbuf_tensor("prod", [P, D], F32))
            s_pads, s_edges, s_const, s_et, s_etout = (sem(n) for n in (
                "edge_pads_set", "edges_loaded", "constants_made", "edge_table_made", "edge_table_stored"))
            s_w, s_dve, s_cnt, s_cntps, s_vidx, s_vg, s_rel, s_relout, s_tr, s_trc, s_wt = (sem(n) for n in (
                "weights_loaded", "setup_vector_steps", "counts_made", "counts_summed", "visit_chunks_known",
                "visits_gathered", "visit_rows_made", "visit_rows_stored", "visit_transposed",
                "visit_copied", "gate_transposed"))
            s_tile = sem("visit_tiles_known")
            s_ab = sem("attention_vectors_loaded")
            full = E // (CG * P)
            rest = E - full * CG * P
            NVEC = 6
            vec_in = [b1, g1, beta1, b2, g2, beta2]
            ab_in = [a_src1.rearrange("h c -> (h c)"), a_dst1.rearrange("h c -> (h c)"),
                     a_src2.rearrange("h c -> (h c)"), a_dst2.rearrange("h c -> (h c)")]

            with nc.Block() as block:
                @block.sync
                def _(sp):
                    sp.wait_ge(s_pads, 2)
                    for stage, arr in ((dstage, dst), (sstage, src)):
                        sp.dma_start(stage[0:full, :], arr[0:full * CG * P].rearrange("(p k) -> p k", k=CG * P)).then_inc(s_edges, 16)
                        sp.dma_start(stage[full:full + 1, 0:rest], arr[full * CG * P:E].rearrange("(a k) -> a k", a=1)).then_inc(s_edges, 16)
                    for i, a in enumerate(ab_in):
                        sp.dma_start(ab[:, i, :], a.rearrange("(a k) -> a k", a=1).to_broadcast([P, D])).then_inc(s_ab, 16)
                    for w, dest in ((W1, Wc[0]), (W2, Wc[1])):
                        sp.dma_start(dest[:], w.rearrange("(k p) n -> p k n", p=P)).then_inc(s_ab, 16)
                    sp.dma_start(gnat[:], gate_w).then_inc(s_w, 16)
                    sp.dma_start(hbn[0:4, :], sb1.rearrange("(k p) -> k p", p=P)).then_inc(s_w, 16)
                    sp.dma_start(hbn[4:12, :], fb1).then_inc(s_w, 16)
                    sp.dma_start(sw1_s[:], sw1.rearrange("(k p) n -> p k n", p=P)).then_inc(s_w, 16)
                    sp.dma_start(sw2_s[:], sw2.rearrange("(k p) n -> p k n", p=P)).then_inc(s_w, 16)
                    sp.dma_start(w2_s[:], w2.rearrange("e p n -> p e n")).then_inc(s_w, 16)
                    for k in range(KT):
                        sp.dma_start(w1_s[:, k], w1[:, k * P:(k + 1) * P, :].rearrange("e p n -> p e n")).then_inc(s_w, 16)
                    sp.dma_start(b2c[0:NE, :], fb2).then_inc(s_w, 16)
                    sp.dma_start(b2c[NE:NE + 1, :], sb2.rearrange("(a k) -> a k", a=1)).then_inc(s_w, 16)
                    for i, a in enumerate(vec_in):
                        sp.dma_start(vecs[:, i, :], a.rearrange("(a k) -> a k", a=1).to_broadcast([P, D])).then_inc(s_w, 16)
                    sp.wait_ge(s_w, 16 * (12 + NVEC))
                    sp.wait_ge(s_ab, 16 * 6)

                @block.gpsimd
                def _(pool):
                    nc.gpsimd.memset(ones[:], 1.0).then_inc(s_const, 1)
                    nc.gpsimd.memset(zero_b[:], 0.0).then_inc(s_const, 1)
                    nc.gpsimd.iota(iota_n[:], pattern=[[-1, P]], base=0, channel_multiplier=0, allow_small_or_imprecise_dtypes=True).then_inc(s_const, 1)
                    nc.gpsimd.iota(iota_p[:], pattern=[[0, 1]], base=0, channel_multiplier=1, allow_small_or_imprecise_dtypes=True).then_inc(s_const, 1)
                    nc.gpsimd.iota(vnum[:], pattern=[[P, VG]], base=0, channel_multiplier=1, allow_small_or_imprecise_dtypes=True).then_inc(s_const, 1)
                    pool.wait_ge(s_const, 5)
                    nc.gpsimd.affine_select(out=ident[:], in_=ones[:], compare_op=ALU.is_equal, fill=0.0, base=0, pattern=[[1, P]], channel_multiplier=-1).then_inc(s_const, 1)
                    nc.gpsimd.affine_select(out=sel[:], in_=ones[0:NE + 1, :].rearrange("p (a k) -> p a k", a=1).to_broadcast([NE + 1, NE, P]), compare_op=ALU.is_equal, fill=0.0, base=0, pattern=[[1, NE], [0, P]], channel_multiplier=-1).then_inc(s_const, 1)
                    nc.gpsimd.affine_select(out=less[:], in_=ones[:, 0:NE * NE].rearrange("p (a k) -> p a k", a=NE), compare_op=ALU.is_gt, fill=0.0, base=0, pattern=[[1, NE], [-1, NE]], channel_multiplier=0).then_inc(s_const, 1)
                    pool.wait_ge(s_etout, 16)
                    pool.wait_ge(s_vidx, 1)
                    for k in range(VG):
                        nc.gpsimd.indirect_dma_start(vt[:, k, :], None, edge_tab, bass.IndirectOffsetOnAxis(ap=vt_ci[:, k:k + 1], axis=0)).then_inc(s_vg, 16)

                @block.vector
                def _(dve):
                    st = Steps(dve, s_dve)
                    v = nc.vector
                    v.memset(dstage[:], int(OUTSIDE)).then_inc(s_pads, 1)
                    v.memset(sstage[:], 0).then_inc(s_pads, 1)
                    dve.wait_ge(s_edges, 64)
                    df = et[:, :, 0:P]
                    st.link(v.tensor_single_scalar(dtile[:], dstage[:], 7, ALU.arith_shift_right))
                    st.link(v.tensor_copy(dtile_b[:], dtile[:]))
                    v.tensor_copy(et[:, :, P:2 * P], sstage[:].rearrange("p (c k) -> p c k", k=P)).then_inc(s_et, 1)
                    st.link(v.tensor_copy(df, dstage[:].rearrange("p (c k) -> p c k", k=P)))
                    dve.sem_inc(s_et, 1)
                    for t in range(1, NT + 1):
                        v.tensor_scalar(junk[:], dtile_b[:], float(t), 0.0, ALU.is_lt, ALU.add, accum_out=cnt[:, t:t + 1]).then_inc(s_cnt, 1)
                        dve.wait_ge(s_cnt, t)
                    v.memset(cnt[:, 0:1], 0.0).then_inc(s_cnt, 1)
                    dve.wait_ge(s_cntps, 1)
                    first, c0, last_, c1, nvis, nquad, qe, dd = f
                    T1 = NT + 1
                    st.link(v.tensor_copy(first[:, 0:T1], small_ps[:, 0:T1]))
                    st.link(v.tensor_copy(n_i[0][:, 0:T1], first[:, 0:T1]))
                    st.link(v.tensor_scalar(last_[:, 0:NT], first[:, 1:T1], -1.0, None, ALU.add))
                    st.link(v.tensor_copy(n_i[1][:, 0:NT], last_[:, 0:NT]))
                    st.link(v.tensor_single_scalar(n_i[2][:, 0:T1], n_i[0][:, 0:T1], 7, ALU.arith_shift_right))
                    st.link(v.tensor_single_scalar(n_i[3][:, 0:NT], n_i[1][:, 0:NT], 7, ALU.arith_shift_right))
                    st.link(v.tensor_copy(c0[:, 0:T1], n_i[2][:, 0:T1]))
                    st.link(v.tensor_copy(c1[:, 0:NT], n_i[3][:, 0:NT]))
                    st.link(v.tensor_tensor(nvis[:, 0:NT], c1[:, 0:NT], c0[:, 0:NT], ALU.subtract))
                    st.link(v.tensor_scalar(nvis[:, 0:NT], nvis[:, 0:NT], 1.0, 1.0, ALU.add, ALU.max))
                    st.link(v.tensor_scalar(nvis[:, 0:NT], nvis[:, 0:NT], 3.0, None, ALU.add))
                    st.link(v.tensor_copy(n_i[0][:, 0:NT], nvis[:, 0:NT]))
                    st.link(v.tensor_single_scalar(n_i[1][:, 0:NT], n_i[0][:, 0:NT], 2, ALU.arith_shift_right))
                    st.link(v.tensor_copy(nquad[:, 0:NT], n_i[1][:, 0:NT]))
                    st.link(v.memset(qe[:], 0.0))
                    st.link(v.memset(last_[:], 0.0))
                    st.link(v.tensor_tensor_scan(qe[:, 1:T1], nquad[:, 0:NT], last_[:, 0:NT], 0.0, ALU.add, ALU.add))
                    st.link(v.tensor_scalar(first[:, 0:1], qe[:, NT:T1], 3.0, None, ALU.add))
                    st.link(v.tensor_copy(n_i[0][:, 0:1], first[:, 0:1]))
                    st.link(v.tensor_single_scalar(n_i[1][:, 0:1], n_i[0][:, 0:1], 2, ALU.arith_shift_right))
                    st.link(v.tensor_copy(first[:, 0:1], n_i[1][:, 0:1]))
                    st.link(v.tensor_scalar(qe[:, NT:T1], first[:, 0:1], 4.0, None, ALU.mult))
                    st.link(v.tensor_copy(q_end[:, 0:T1], qe[:, 0:T1]))
                    st.link(v.tensor_copy(q_end[:, T1:T1 + 1], first[:, 0:1]))
                    dve.wait_ge(s_const, 5)
                    st.link(v.tensor_tensor(big3[:, :, 0:NT - 1], vnum[:, 0:QG].rearrange("p (v a) -> p v a", a=1).to_broadcast([P, QG, NT - 1]),
                                            qe[:, 1:NT].rearrange("p (a t) -> p a t", a=1).to_broadcast([P, QG, NT - 1]), ALU.is_ge))
                    st.link(v.tensor_reduce(qt[:], big3[:, :, 0:NT - 1], AX.X, ALU.add))
                    dve.wait_ge(s_const, 6)
                    for k in range(QG):
                        v.tensor_scalar(qdiag[:, k * P:(k + 1) * P], ident[:], qt[:, k:k + 1], None, ALU.mult).then_inc(s_tile, 1)
                    st.link(v.tensor_scalar(qe[:, 0:T1], qe[:, 0:T1], 4.0, None, ALU.mult))
                    st.link(v.tensor_tensor(dd[:, 0:NT], c0[:, 0:NT], qe[:, 0:NT], ALU.subtract))
                    st.link(v.tensor_tensor(nvis[:, 1:NT], dd[:, 1:NT], dd[:, 0:NT - 1], ALU.subtract))
                    vb = vnum[:].rearrange("p (v a) -> p v a", a=1).to_broadcast([P, VG, NT - 1])
                    qb = qe[:, 1:NT].rearrange("p (a t) -> p a t", a=1).to_broadcast([P, VG, NT - 1])
                    db = nvis[:, 1:NT].rearrange("p (a t) -> p a t", a=1).to_broadcast([P, VG, NT - 1])
                    st.link(v.tensor_tensor(big[:, :, 0:NT - 1], vb, qb, ALU.is_ge))
                    st.link(v.tensor_reduce(vt_t[:], big[:, :, 0:NT - 1], AX.X, ALU.add))
                    st.link(v.tensor_tensor(big2[:, :, 0:NT - 1], big[:, :, 0:NT - 1], db, ALU.mult))
                    st.link(v.tensor_reduce(vt_c[:], big2[:, :, 0:NT - 1], AX.X, ALU.add))
                    st.link(v.tensor_tensor(vt_c[:], vt_c[:], vnum[:], ALU.add))
                    st.link(v.tensor_scalar(vt_c[:], vt_c[:], 0.0, float(NCH), ALU.max, ALU.min))
                    v.tensor_copy(vt_ci[:], vt_c[:]).then_inc(s_vidx, 1)
                    st.link(v.tensor_scalar(vt_o[:], vt_t[:], -float(P), None, ALU.mult))
                    dve.wait_ge(s_tr, 1)
                    st.link(v.tensor_copy(quad_tile[:], hid0_ps[0:1, 0:QG * P]))
                    dve.wait_ge(s_vg, 16 * VG)
                    for k in range(VG):
                        v.tensor_scalar(vt[:, k, 0:P], vt[:, k, 0:P], vt_o[:, k:k + 1], None, ALU.add).then_inc(s_rel, 1)
                    dve.wait_ge(s_rel, VG)
                    v.tensor_copy(relb[:], vt[:, :, 0:P]).then_inc(s_rel, 1)
                    for k in range(VG):
                        dve.wait_ge(s_trc, k + 1)
                        v.tensor_scalar(relN[:, k * P:(k + 1) * P], (tr_ps, dense_ps)[k % 2][:, 0:P], -1.0, None, ALU.mult).then_inc(s_cnt, 1)
                        v.tensor_copy(srcT[:, k * P:(k + 1) * P], (tr_ps, dense_ps)[k % 2][:, P:2 * P]).then_inc(s_cnt, 1)
                    dve.wait_ge(s_ab, 96)
                    for i in range(2):
                        nh = (H, 1)[i]
                        for k in range(KT):
                            for j in range(2):
                                st.link(v.tensor_tensor(prod[:], Wc[i][:, k, :], ab[:, 2 * i + j, :], ALU.mult))
                                st.link(v.tensor_reduce(WA[i][:, k, j * nh:(j + 1) * nh], prod[:].rearrange("p (h c) -> p h c", h=nh), AX.X, ALU.add))
                    dve.wait_ge(s_wt, 1)
                    st.link(v.tensor_copy(gateT[:], acc_ps[:, 0:KT * NE].rearrange("p (k e) -> p k e", k=KT)))
                    st.link(v.tensor_copy(hb[:], nodes_ps[:, 0:12]))

                @block.scalar
                def _(act):
                    act.wait_ge(s_et, 2)
                    act.dma_start(edge_tab.rearrange("(p c) k -> p c k", c=CG), et[:]).then_inc(s_etout, 16)
                    act.wait_ge(s_rel, VG + 1)
                    act.dma_start(rel_tab.rearrange("(k p) e -> p k e", p=P), relb[:]).then_inc(s_relout, 16)
                    act.wait_ge(s_relout, 16)

                @block.tensor
                def _(pe):
                    m = nc.tensor
                    pe.wait_ge(s_cnt, NT + 1)
                    pe.wait_ge(s_const, 8)
                    m.matmul(small_ps[:, 0:NT + 1], ones[:], cnt[:, 0:NT + 1], start=True, stop=True).then_inc(s_cntps, 1)
                    pe.wait_ge(s_tile, QG)
                    m.matmul(hid0_ps[:, 0:QG * P], ones[:], qdiag[:], start=True, stop=True).then_inc(s_tr, 1)
                    pe.wait_ge(s_rel, VG)
                    for k in range(VG):
                        bank = (tr_ps, dense_ps)[k % 2]
                        if k >= 2:
                            pe.wait_ge(s_cnt, NT + 1 + 2 * (k - 1))
                        m.transpose(bank[:, 0:P], vt[:, k, 0:P], ident[:])
                        m.transpose(bank[:, P:2 * P], vt[:, k, P:2 * P], ident[:]).then_inc(s_trc, 1)
                    pe.wait_ge(s_w, 16 * (12 + NVEC))
                    for k in range(KT):
                        m.transpose(acc_ps[:, k * NE:(k + 1) * NE], gnat[:, k * P:(k + 1) * P], ident[0:NE, 0:NE])
                    m.transpose(nodes_ps[:, 0:12], hbn[:], ident[0:12, 0:12]).then_inc(s_wt, 1)

        def rsqrt_steps(st, var, o):
            v = nc.vector
            half, y, t1 = (sm[:, o + i:o + i + 1] for i in range(3))
            st.link(v.tensor_scalar(half, var, EPS, 0.5, ALU.add, ALU.mult))
            st.link(v.tensor_scalar(y.bitcast(I32), half.bitcast(I32), -0.5, MAGIC_MINUS, ALU.mult, ALU.add))
            for _ in range(3):
                st.link(v.tensor_scalar(t1, y, y, half, ALU.mult, ALU.mult))
                st.link(v.scalar_tensor_tensor(y, t1, 1.5, y, ALU.subtract, ALU.mult))
            return y

        def bn_row(st, data, o):
            st.link(nc.vector.bn_stats(bn[:], data))
            st.eng.sem_inc(s_stats, 1)
            st.link(nc.vector.bn_aggr(sm[:, o:o + 2], bn[:]))

        def bn_chain(st, o):
            y = rsqrt_steps(st, sm[:, o + 1:o + 2], o + 2)
            st.link(nc.vector.scalar_tensor_tensor(sm[:, o + 5:o + 6], sm[:, o:o + 1], -1.0, y, ALU.mult, ALU.mult))
            return sm[:, o:o + 1], y, sm[:, o + 5:o + 6]

        def bn_steps(st, data, o):
            bn_row(st, data, o)
            return bn_chain(st, o)

        BN = 2 + 8 + 1

        def project_stage():
            s_x = [sem("x_loaded_even"), sem("x_loaded_odd")]
            s_st = [sem("h_stored_even"), sem("h_stored_odd")]
            s_v, s_xn, s_tp, s_tc, s_mm, s_ho = (sem(n) for n in (
                "proj_vector_steps", "xn_made", "xn_transposed", "xT_copied", "h_made", "h_copied"))
            xin = [sbs(f"xin{i}", [P, D]) for i in range(2)]
            xn = [sbs(f"xn{i}", [P, D]) for i in range(2)]
            xTs = [sbs(f"xTp{i}", [P, KT, P]) for i in range(2)]
            ho = [sbs(f"ho{i}", [P, RW]) for i in range(2)]
            KV = BN + 2
            HALF = (NT - 1) // 2

            with nc.Block() as block:
                @block.sync
                def _(sp):
                    def load(i, k, n=P):
                        sp.dma_start(xin[k][0:n, :], tile_rows(x, 2 * i + k, n)).then_inc(s_x[k], 16)

                    load(0, 0)
                    load(0, 1)
                    with sp.Fori(0, HALF - 1) as i:
                        for k in range(2):
                            sp.wait_ge(s_xn, 2 * i + k + 1)
                            load(i + 1, k)
                    sp.wait_ge(s_xn, NT - 2)
                    load(HALF, 0, LAST)

                @block.gpsimd
                def _(pool):
                    def store(i, k, n=P):
                        pool.wait_ge(s_ho, 2 * i + k + 1)
                        pool.dma_start(tile_rows(h_tab[0], 2 * i + k, n), ho[k][0:n, :]).then_inc(s_st[k], 16)
                    with pool.Fori(0, HALF) as i:
                        store(i, 0)
                        store(i, 1)
                    store(HALF, 0, LAST)
                    pool.wait_ge(s_st[0], 16 * (HALF + 1))
                    pool.wait_ge(s_st[1], 16 * HALF)

                @block.vector
                def _(dve):
                    v = nc.vector

                    def body(i, k):
                        t = 2 * i + k
                        st = Steps(dve, s_v, KV * t)
                        dve.wait_ge(s_x[k], 16 * (i + 1))
                        mean, rstd, shift = bn_steps(st, xin[k][:], 0)
                        st.link(v.tensor_copy(stats[:, bass.ds(t, 1), 0:1], shift))
                        st.link(v.tensor_copy(stats[:, bass.ds(t, 1), 1:2], rstd))
                        assert st.n == KV
                        need(dve, s_tp, t - 1)
                        v.tensor_scalar(xn[k][:], xin[k][:], mean, rstd, ALU.subtract, ALU.mult).then_inc(s_xn, 1)
                    body(0, 0)
                    body(0, 1)
                    with dve.Fori(1, HALF) as i:
                        body(i, 0)
                        body(i, 1)
                    body(HALF, 0)

                @block.tensor
                def _(pe):
                    m = nc.tensor

                    def turn(t, k):
                        pe.wait_ge(s_xn, t + 1)
                        need(pe, s_tc, t)
                        for j in range(KT):
                            ins = m.transpose(tr_ps[:, j * P:(j + 1) * P], xn[k][:, j * P:(j + 1) * P], ident[:])
                        ins.then_inc(s_tp, 1)

                    def project(t, k):
                        pe.wait_ge(s_tc, t + 1)
                        need(pe, s_ho, t - 1)
                        bank, small = (dense_ps, small_ps) if k == 0 else (hid0_ps, hid1_ps)
                        for j in range(KT):
                            m.matmul(bank[:], xTs[k][:, j, :], Wc[0][:, j, :], start=(j == 0), stop=(j == KT - 1))
                        for j in range(KT):
                            ins = m.matmul(small[:, 0:16], xTs[k][:, j, :], WA[0][:, j, :], start=(j == 0), stop=(j == KT - 1))
                        ins.then_inc(s_mm, 1)

                    def both(i):
                        turn(2 * i + 1, 1)
                        project(2 * i, 0)
                        turn(2 * i + 2, 0)
                        project(2 * i + 1, 1)
                    turn(0, 0)
                    both(0)
                    with pe.Fori(1, HALF) as i:
                        both(i)
                    project(NT - 1, 0)

                @block.scalar
                def _(act):
                    a = nc.scalar

                    def copy_t(t, k):
                        act.wait_ge(s_tp, t + 1)
                        need(act, s_mm, t - 1)
                        a.copy(xTs[k][:], tr_ps[:].rearrange("p (k n) -> p k n", k=KT)).then_inc(s_tc, 1)

                    def copy_h(i, k):
                        t = 2 * i + k
                        bank, small = (dense_ps, small_ps) if k == 0 else (hid0_ps, hid1_ps)
                        act.wait_ge(s_mm, t + 1)
                        need(act, s_st[k], 16 * i)
                        a.copy(ho[k][:, 0:D], bank[:])
                        a.copy(ho[k][:, D:D + 8], small[:, 0:8])
                        a.copy(AS[:, bass.ds(t, 1), :], small[:, 0:8].rearrange("p (a h) -> p a h", a=1))
                        a.copy(AD[:, bass.ds(t, 1), :], small[:, 8:16].rearrange("p (a h) -> p a h", a=1)).then_inc(s_ho, 1)

                    def both(i):
                        copy_t(2 * i + 1, 1)
                        copy_h(i, 0)
                        copy_t(2 * i + 2, 0)
                        copy_h(i, 1)
                    copy_t(0, 0)
                    both(0)
                    with act.Fori(1, HALF) as i:
                        both(i)
                    copy_h(HALF, 0)

        def reference_stage(c, nh):
            n = lambda w: f"{w}{c + 1}"
            (s_r, s_m, s_p, s_z, s_e, s_free, s_idx, s_tk, s_rel, s_diag, s_rep) = (sem(n(w)) for w in (
                "ref_steps", "partition_max_made", "max_made", "own_logits_made", "own_weights_made",
                "max_buffers_free", "max_indices_copied", "max_slot_taken", "max_rel_landed", "max_diagonals_made",
                "max_values_spread"))
            s_rows = sem(n("max_rows_landed"))
            u, r, q, w, M = (sbs(f"ref{i}_{c}", [P, NT, 8]) for i in range(5))
            span = sbs(n("span"), [P, 16])
            quads_i = sbs(n("quads_to_do"), [P, 1], I32)
            rows = sbs(n("max_rows"), [P, 4, RW])
            relB = sbs(n("max_rel"), [P, 4 * P], BF16)
            idx = sbs(n("max_idx"), [P, 4], I32)
            pen, masked = sbs(n("pen"), [P, 4 * P]), sbs(n("masked"), [P, 4 * P])
            diag = sbs(n("diag"), [P, 4 * P])
            mx = sbs(n("mx"), [P, 1])
            H_ = slice(0, nh)

            with nc.Block() as block:
                @block.vector
                def _(dve):
                    st, v = Steps(dve, s_r), nc.vector
                    a_s = AS[:, :, H_].rearrange("p t h -> p h t")
                    st.link(v.memset(amaxp[:], 0.0))
                    st.link(v.tensor_reduce(amaxp[:, H_], a_s, AX.X, ALU.max))
                    st.link(v.tensor_reduce(span[:, H_], a_s, AX.X, ALU.min))
                    v.tensor_scalar(amaxp[:, 8:8 + nh], span[:, H_], -1.0, None, ALU.mult).then_inc(s_m, 1)
                    dve.wait_ge(s_p, 1)
                    st.link(v.tensor_tensor(span[:, H_], amax[:, H_], amax[:, 8:8 + nh], ALU.add))
                    st.link(v.tensor_reduce(span[:, 8:9], span[:, H_], AX.X, ALU.max))
                    st.link(v.tensor_scalar(span[:, 9:10], span[:, 8:9], SPAN, None, ALU.is_gt))
                    st.link(v.tensor_scalar(span[:, 10:11], span[:, 9:10], -1.0, 1.0, ALU.mult, ALU.add))
                    st.link(v.tensor_scalar(span[:, H_], amax[:, H_], span[:, 10:11], None, ALU.mult))
                    mb = span[:, H_].rearrange("p (a h) -> p a h", a=1).to_broadcast([P, NT, nh])
                    st.link(v.scalar_tensor_tensor(M[:, :, H_], AS[:, :, H_], span[:, 9:10], mb, ALU.mult, ALU.add))
                    st.link(v.tensor_copy(span[:, 11:12], q_end[:, NT:NT + 1]))
                    st.link(v.tensor_scalar(span[:, 12:13], span[:, 11:12], span[:, 9:10], None, ALU.mult))
                    st.link(v.tensor_copy(quads_i[:], span[:, 12:13]))

                @block.gpsimd
                def _(pool):
                    pool.wait_ge(s_m, 1)
                    nc.gpsimd.partition_all_reduce(amax[:], amaxp[:], P, bass.bass_isa.ReduceOp.max).then_inc(s_p, 1)

            K0, KM = 12, 2 + 2 * nh
            with nc.Block() as block:
                def each_quad(eng, body):
                    todo = eng.value_load(quads_i[0:1, 0:1], min_val=0, max_val=QMAX)
                    with eng.If(todo > 0):
                        with eng.Fori(0, todo) as i:
                            body(i)

                @block.gpsimd
                def _(pool):
                    def quad(i):
                        pool.wait_ge(s_free, i + 1)
                        nc.gpsimd.tensor_copy(idx[:], srcT[:, bass.ds(4 * i, 4)]).then_inc(s_idx, 1)
                        pool.wait_ge(s_idx, i + 1)
                        pool.sem_inc(s_tk, 1)
                        for k in range(4):
                            nc.gpsimd.indirect_dma_start(rows[:, k, :], None, h_tab[c],
                                                         bass.IndirectOffsetOnAxis(ap=idx[:, k:k + 1], axis=0)).then_inc(s_rows, 16)
                        pool.wait_ge(s_rows, 64 * i + 64)
                        pool.sem_inc(s_tk, 1)
                    each_quad(pool, quad)

                @block.sync
                def _(sp):
                    def quad(i):
                        sp.wait_ge(s_free, i + 1)
                        sp.dma_start(relB[:], rel_tab[bass.ds(4 * i, 4), :].rearrange("(a v) e -> a (v e)", a=1).to_broadcast([P, 4 * P])).then_inc(s_rel, 16)
                        sp.wait_ge(s_rel, 16 * i + 16)
                        sp.sem_inc(s_tk, 1)
                    each_quad(sp, quad)

                @block.tensor
                def _(pe):
                    def quad(i):
                        for h in range(nh):
                            pe.wait_ge(s_diag, nh * i + h + 1)
                            nc.tensor.matmul(acc_ps[:], ones[:], diag[:], start=True, stop=True).then_inc(s_rep, 1)
                    each_quad(pe, quad)

                @block.vector
                def _(dve):
                    v = nc.vector
                    dve.sem_inc(s_free, 1)
                    def quad(i):
                        tile = dve.value_load(quad_tile[0:1, bass.ds(i, 1)], min_val=0, max_val=NT - 1)
                        st = Steps(dve, s_r, KM * i + K0)
                        dve.wait_ge(s_rel, 16 * i + 16)
                        st.link(v.tensor_scalar(masked[:], relB[:], iota_p[:], None, ALU.is_equal))
                        st.link(v.tensor_scalar(pen[:], masked[:], 1.0, 1e38, ALU.subtract, ALU.mult))
                        dve.wait_ge(s_rows, 64 * i + 64)
                        for h in range(nh):
                            for k in range(4):
                                ins = v.tensor_scalar(diag[:, k * P:(k + 1) * P], ident[:], rows[:, k, D + h:D + h + 1], None, ALU.mult)
                            ins.then_inc(s_diag, 1)
                            dve.wait_ge(s_rep, nh * i + h + 1)
                            st.link(v.tensor_tensor(masked[:], pen[:], acc_ps[:], ALU.add))
                            st.link(v.tensor_reduce(mx[:], masked[:], AX.X, ALU.max))
                            m_h = M[:, bass.ds(tile, 1), h:h + 1].rearrange("p a h -> p (a h)")
                            ins = v.tensor_tensor(m_h, m_h, mx[:], ALU.max)
                        assert st.n == KM, (st.n, KM)
                        ins.then_inc(s_free, 1)
                        dve.wait_ge(s_free, i + 2)
                    each_quad(dve, quad)

            with nc.Block() as block:
                @block.vector
                def _(dve):
                    v = nc.vector
                    st = Steps(dve, s_z)
                    st.link(v.tensor_tensor(u[:, :, H_], AD[:, :, H_], M[:, :, H_], ALU.add))
                    st.link(v.scalar_tensor_tensor(r[:, :, H_], u[:, :, H_], SLOPE, u[:, :, H_], ALU.mult, ALU.max))
                    for o, val in ((0, AD), (nh, r)):
                        st.link(v.tensor_copy(NRb[:, :, 0, o:o + nh], val[:, :, H_]))
                        st.link(v.tensor_tensor(q[:, :, H_], val[:, :, H_], NRb[:, :, 0, o:o + nh], ALU.subtract))
                        st.link(v.tensor_copy(NRb[:, :, 1, o:o + nh], q[:, :, H_]))
                        st.link(v.tensor_tensor(NRb[:, :, 2, o:o + nh], q[:, :, H_], NRb[:, :, 1, o:o + nh], ALU.subtract))
                    st.link(v.tensor_tensor(u[:, :, H_], AS[:, :, H_], AD[:, :, H_], ALU.add))
                    st.link(v.scalar_tensor_tensor(q[:, :, H_], u[:, :, H_], SLOPE, u[:, :, H_], ALU.mult, ALU.max))
                    st.link(v.tensor_tensor(w[:, :, H_], q[:, :, H_], r[:, :, H_], ALU.subtract))
                    st.link(v.tensor_scalar(u[:, :, H_], w[:, :, H_], 0.0, None, ALU.min))

                @block.scalar
                def _(act):
                    act.wait_ge(s_z, 14)
                    nc.scalar.activation(ES[:, :, 0:nh], u[:, :, 0:nh], ACT.Exp).then_inc(s_e, 1)
                    act.wait_ge(s_e, 1)

        def conv_stage(c, nh):
            first = c == 0
            n = lambda w: f"{w}{c + 1}"
            s_row = [sem(n(f"rows_of_{w}_quads")) for w in ("even", "odd")]
            s_rb = [sem(n(f"rel_landed_slot{k}_")) for k in range(2)]
            (s_rows, s_rel, s_ST, s_adE, s_z, s_e, s_S, s_sq, s_msg, s_main, s_evac, s_idx, s_taken,
             s_pv) = (sem(n(w)) for w in (
                 "rows_landed", "rel_landed", "onehotT_made", "node_values_made", "logits_made", "weights_made",
                 "onehot_made", "squares_made", "messages_made", "visits_done", "acc_copied", "indices_copied",
                 "slots_taken", "quad_vector_steps"))
            s_acc = [sem(n("acc_stored_even")), sem(n("acc_stored_odd"))]
            rows = sbs(n("rows"), [P, RING, RW])
            relB = sbs(n("relB"), [P, 2, 4 * P], BF16)
            idx = sbs(n("idx"), [P, RING], I32)
            ST = sbs(n("ST"), [P, 4, P], BF16)
            S = [sbs(n(f"S{k}_"), [P, P]) for k in range(4)]
            sq = sbs(n("sq"), [P, 4, P]) if first else None
            msg = [sbs(n(f"msg{k}_"), [P, RW]) for k in range(4)] if first else None
            z1, z2, z3, z4 = (sbs(n(f"z{k}_"), [P, 4, 8]) for k in range(4))
            e_s = sbs(n("e_s"), [P, 2, 4, 8])
            e_w = sbs(n("e_w"), [P, 4, 8]) if first else None
            accS = [sbs(n(f"accS{k}_"), [P, RW]) for k in range(2)]
            HW = RW // 2
            acc_banks = ((acc_ps, small_ps), (tr_ps, dense_ps))
            HALF = (NT - 1) // 2

            def bounds(eng, t):
                a = eng.value_load(q_end[0:1, bass.ds(t, 1)], min_val=0, max_val=QMAX)
                b = eng.value_load(q_end[0:1, bass.ds(t + 1, 1)], min_val=1, max_val=QMAX)
                return a, b

            def tiles(eng, tile):
                for t in range(4):
                    tile(t // 2, t % 2)
                with eng.Fori(2, HALF) as i:
                    tile(i, 0)
                    tile(i, 1)
                tile(HALF, 0)

            def heads(ap):
                return ap.rearrange("p (h c) -> p h c", h=nh)

            def spread(ap):
                return ap.rearrange("p (h a) -> p h a", a=1).to_broadcast([P, nh, D // nh])

            with nc.Block() as block:
                @block.gpsimd
                def _(pool):
                    turns = pool.value_load(q_end[0:1, NT + 1:NT + 2], min_val=2, max_val=QMAX // 4)
                    used = s_msg if first else s_main

                    def landed(i, q):
                        pool.wait_ge(s_row[q % 2], 64 * (2 * i + q // 2 + 1))
                        pool.sem_inc(s_rows, 1)

                    def indices(i, q):
                        to = 4 * (q % 4)
                        nc.gpsimd.tensor_copy(idx[:, to:to + 4], srcT[:, bass.ds(RING * i + 4 * q, 4)]).then_inc(s_idx, 1)

                    def turn(i):
                        for q in range(4):
                            pool.wait_ge(s_idx, 4 * i + q + 1)
                            pool.wait_ge(used, RING * i + 4 * q + 4)
                            pool.sem_inc(s_taken, 1)
                            indices(i, q + 1)
                            for k in range(4 * q, 4 * q + 4):
                                nc.gpsimd.indirect_dma_start(
                                    rows[:, k, :], None, h_tab[c],
                                    bass.IndirectOffsetOnAxis(ap=idx[:, k:k + 1], axis=0)).then_inc(s_row[q % 2], 16)
                            if q or not isinstance(i, int):
                                landed(i, q - 1)
                    indices(0, 0)
                    turn(0)
                    with pool.Fori(1, turns) as i:
                        turn(i)
                    landed(turns, -1)

                @block.sync
                def _(sp):
                    pairs = 2 * sp.value_load(q_end[0:1, NT + 1:NT + 2], min_val=2, max_val=QMAX // 4)

                    def pair(i):
                        for k in range(2):
                            need(sp, s_ST, 2 * i + k - 1)
                            sp.dma_start(relB[:, k, :], rel_tab[bass.ds(8 * i + 4 * k, 4), :].rearrange("(a v) e -> a (v e)", a=1).to_broadcast([P, 4 * P])).then_inc(s_rb[k], 16)
                            if k or not isinstance(i, int):
                                sp.wait_ge(s_rb[1 - k], 16 * i + (16 if k else 0))
                                sp.sem_inc(s_rel, 1)
                    pair(0)
                    with sp.Fori(1, pairs + 1) as i:
                        pair(i)
                    sp.wait_ge(s_rb[1], 16 * pairs + 16)
                    sp.sem_inc(s_rel, 1)

                @block.vector
                def _(dve):
                    v = nc.vector
                    KQ = 3

                    def front(u):
                        dve.wait_ge(s_rel, u + 1)
                        need(dve, s_adE, u)
                        v.tensor_scalar(ST[:].rearrange("p v e -> p (v e)"), relB[:, bass.ds(u % 2, 1), :].rearrange("p a k -> p (a k)"), iota_p[:], None, ALU.is_equal).then_inc(s_ST, 1)

                    def quad(u):
                        st = Steps(dve, s_pv, KQ * u)
                        slot = (u % 4) * 4
                        adE = nodes_ps[:, 0:64].rearrange("p (v k) -> p v k", v=4)
                        dve.wait_ge(s_adE, u + 1)
                        dve.wait_ge(s_rows, u + 1)
                        st.link(v.tensor_tensor(z1[:, :, 0:nh], rows[:, bass.ds(slot, 4), D:D + nh], adE[:, :, 0:nh], ALU.add))
                        st.link(v.scalar_tensor_tensor(z2[:, :, 0:nh], z1[:, :, 0:nh], SLOPE, z1[:, :, 0:nh], ALU.mult, ALU.max))
                        st.link(v.tensor_tensor(z3[:, :, 0:nh], z2[:, :, 0:nh], adE[:, :, nh:2 * nh], ALU.subtract))
                        assert st.n == KQ
                        v.tensor_scalar(z4[:, :, 0:nh], z3[:, :, 0:nh], 0.0, None, ALU.min).then_inc(s_z, 1)
                        front(u + 1)
                        dve.wait_ge(s_e, u + 1)
                        for k in range(4):
                            dve.wait_ge(s_main, 4 * u + k + 1 + RING - 4)
                            e_k = e_s[:, bass.ds(u % 2, 1), k, 0:nh].rearrange("p a h -> p (a h)")
                            if first:
                                v.tensor_tensor(heads(msg[k][:, 0:D]), heads(rows[:, bass.ds(slot + k, 1), 0:D].rearrange("p a n -> p (a n)")),
                                                spread(e_k), ALU.mult).then_inc(s_msg, 1)
                            else:
                                v.tensor_scalar(S[k][:], iota_n[:], relN[:, bass.ds(4 * u + k, 1)], e_k, ALU.is_equal, ALU.mult).then_inc(s_msg, 1)

                    if first:
                        dve.sem_inc(s_msg, RING)
                    front(0)

                    def tile(i, k):
                        a, b = bounds(dve, 2 * i + k)
                        with dve.Fori(a, b) as u:
                            quad(u)
                    tiles(dve, tile)

                @block.scalar
                def _(act):
                    a_ = nc.scalar

                    def squares(u):
                        need(act, s_S, 4 * u)
                        for k in range(4):
                            a_.activation(sq[:, k, :], iota_n[:], ACT.Square, bias=relN[:, bass.ds(4 * u + k, 1)], scale=-1.0).then_inc(s_sq, 1)

                    def quad(u):
                        act.wait_ge(s_z, u + 1)
                        act.wait_ge(s_main, 4 * u - 4 + RING)
                        if first:
                            a_.activation(e_w[:], z4[:], ACT.Exp)
                        a_.activation(e_s[:, bass.ds(u % 2, 1), :, 0:nh].rearrange("p a v h -> p (a v) h"), z4[:, :, 0:nh], ACT.Exp).then_inc(s_e, 1)
                        if first:
                            act.wait_ge(s_sq, 4 * u + 4)
                            act.wait_ge(s_e, u + 1)
                            for k in range(4):
                                act.wait_ge(s_main, 4 * u + k + 1 + RING - 4)
                                a_.copy(msg[k][:, D:RW], e_w[:, k, :])
                                a_.activation(S[k][:], sq[:, k, :], ACT.Relu, bias=ones[:, 0:1], scale=-1.0).then_inc(s_S, 1)
                            squares(u + 1)

                    def evacuate(i, k):
                        t = 2 * i + k
                        act.wait_ge(s_main, act_end[k] * 4 + RING)
                        need(act, s_acc[k], 16 * i)
                        for half, bank in enumerate(acc_banks[k]):
                            a_.copy(accS[k][:, half * HW:(half + 1) * HW], bank[:, 0:HW]).then_inc(s_evac, 1)
                        act.wait_ge(s_evac, 2 * t + 2)
                        act.dma_start(tile_rows(acc_tab, t), accS[k][:]).then_inc(s_acc[k], 16)

                    act_end = [None, None]

                    def tile(i, k):
                        a, b = bounds(act, 2 * i + k)
                        with act.Fori(a, b) as u:
                            quad(u)
                        act_end[1 - k] = a
                        if k:
                            evacuate(i, 0)
                        elif not (isinstance(i, int) and i == 0):
                            evacuate(i - 1, 1)
                        act_end[k] = b
                    if first:
                        squares(0)
                    tiles(act, tile)
                    evacuate(HALF, 0)
                    act.wait_ge(s_acc[0], 16 * (HALF + 1))
                    act.wait_ge(s_acc[1], 16 * HALF)

                @block.tensor
                def _(pe):
                    m = nc.tensor
                    pe.sem_inc(s_main, RING)

                    def front(u):
                        tq = pe.value_load(quad_tile[0:1, bass.ds(u, 1)], min_val=0, max_val=NT - 1)
                        pe.wait_ge(s_ST, u + 1)
                        for k in range(4):
                            for part in range(3):
                                ins = m.matmul(nodes_ps[:, 16 * k:16 * k + 2 * nh], ST[:, k, :], NRb[:, bass.ds(tq, 1), part, 0:2 * nh].rearrange("p a k -> p (a k)"),
                                               start=(part == 0), stop=(part == 2), skip_group_check=True)
                        ins.then_inc(s_adE, 1)

                    def quad(u, banks):
                        front(u + 1)
                        for k in range(4):
                            pe.wait_ge(s_msg, 4 * u + k + 1 + (RING if first else 0))
                            if first:
                                pe.wait_ge(s_S, 4 * u + k + 1)
                            for half, bank in enumerate(banks):
                                cols = slice(half * HW, (half + 1) * HW)
                                rhs = msg[k][:, cols] if first else rows[:, bass.ds((u % 4) * 4 + k, 1), cols].rearrange("p a n -> p (a n)")
                                ins = m.matmul(bank[:, 0:HW], S[k][:], rhs, start=False, stop=False, skip_group_check=True)
                            ins.then_inc(s_main, 1)

                    front(0)

                    def tile(i, k):
                        a, b = bounds(pe, 2 * i + k)
                        need(pe, s_evac, 2 * (2 * i + k - 1))
                        for bank in acc_banks[k]:
                            m.matmul(bank[:, 0:HW], zero_b[:, 0:P], zero_b[:, 0:HW], start=True, stop=False, skip_group_check=True)
                        with pe.Fori(a, b) as u:
                            quad(u, acc_banks[k])
                    tiles(pe, tile)

        def node_stage(c, nh):
            first = c == 0
            DEN = D if first else D + 1
            bias, gain, shift = (vecs[:, 3 * c + i, :] for i in range(3))
            n = lambda w: f"{w}{c + 1}"
            first_only = ("node_h_made", "node_h_copied", "x_layer_norm_made", "ones_set")
            second_only = ("residual_summed", "gate_shifted", "gate_exp_made", "hidden_made", "shared_hidden_used", "experts03_used",
                           "x_normed", "gate_made", "combine_made", "combine_transposed", "combine_copied",
                           "hidden_relu", "weights_spread", "hidden_weighted", "ffn_made", "out_made", "x2_stats_made")
            (s_v, s_nn, s_norm, s_y, s_el, s_mid, s_xl, s_tp, s_tc, s_mm, s_ho, s_g, s_gz, s_ge, s_cw, s_ct,
             s_ctc, s_hid, s_relu, s_crep, s_hs, s_fo, s_out, s_x2n, s_xln,
             s_own, s_sum, s_pl, s_rp, s_mr, s_ones, s_h0u, s_hs1) = (None if w in (second_only if first else first_only) else sem(n(w)) for w in (
                 "node_vector_steps", "node_stats_made", "normed", "affine_made", "elu_parts_made", "x_new_made",
                 "x_normed", "x_transposed", "node_xT_copied", "node_h_made", "node_h_copied", "gate_made",
                 "gate_shifted", "gate_exp_made", "combine_made", "combine_transposed", "combine_copied",
                 "hidden_made", "hidden_relu", "weights_spread", "hidden_weighted", "ffn_made", "out_made",
                 "x2_stats_made", "x_layer_norm_made", "own_loop_made", "residual_summed", "pool_steps",
                 "relu_made", "minus_relu_made", "ones_set", "shared_hidden_used", "experts03_used"))
            s_in = [sem(n("node_inputs_even")), sem(n("node_inputs_odd"))]
            s_res = [sem(n("residual_even")), sem(n("residual_odd"))]
            s_sa = [sem(n("node_store_even")), sem(n("node_store_odd"))]
            s_sb = [sem(n("node_h_store_even")), sem(n("node_h_store_odd"))] if first else None
            two = lambda name, w: [sbs(n(f"{name}{k}_"), [P, w]) for k in range(2)]
            ac, ht, xt = two("ac", RW), two("ht", RW), two("xt", D)
            x1t = None if first else two("x1t", D)
            B1, B2 = two("B1", D), two("B2", D)
            NM, Y, RP, EX, XN = two("NM", D), two("Y", D), two("RP", D), two("EX", D), two("XN", D)
            X1 = two("X1", D)
            smn = [sbs(n(f"smn{k}_"), [P, 2]) for k in range(2)]
            sm2 = [sbs(n(f"sm2{k}_"), [P, 2]) for k in range(2)]
            xT = [sbs(n(f"nxT{k}_"), [P, KT, P]) for k in range(2)]
            ho = two("nho", RW) if first else None
            if not first:
                XL = sbs(n("XL"), [P, D])
                hs = sbs(n("hs"), [P, 2, 4, P])
                cw = [sbs(n(f"cw{k}_"), [P, 16]) for k in range(2)]
                ctr = [sbs(n(f"ctr{k}_"), [NE + 1, P]) for k in range(2)]
                c3 = [sbs(n(f"cmp{i}_"), [P, NE, NE]) for i in range(3)]
                g8 = sbs(n("g8"), [P, 8, 8])
                OUT = two("OUT", D)
            small8 = sbs(n("den8"), [P, 2, 8])
            LAGS = 2
            HALF = (NT - 1) // 2

            def steps(eng, step):
                for s in range(4):
                    step(s // 2, s % 2)
                with eng.Fori(2, HALF - 1) as i:
                    step(i, 0)
                    step(i, 1)
                for s in range(NT - 3, NT + LAGS):
                    step(s // 2, s % 2)

            def at(i, k, back):
                if isinstance(i, int):
                    s = 2 * i + k - back
                    return (s, s // 2, s % 2) if 0 <= s < NT else None
                return (2 * i + k - back, i - (back - k + 1) // 2, (k - back) % 2)

            def heads(ap):
                return ap.rearrange("p (h c) -> p h c", h=nh)

            def spread(ap):
                return ap.rearrange("p (h a) -> p h a", a=1).to_broadcast([P, nh, D // nh])

            def size(t):
                return LAST if isinstance(t, int) and t == NT - 1 else P

            with nc.Block() as block:
                @block.sync
                def _(sp):
                    def load_sums(t, i, k):
                        r = size(t)
                        need(sp, s_nn, t - 1)
                        sp.dma_start(ac[k][:], tile_rows(acc_tab, t)).then_inc(s_in[k], 16)
                        sp.dma_start(ht[k][0:r, :], tile_rows(h_tab[c], t, r)).then_inc(s_in[k], 16)

                    def load_residual(t, i, k):
                        r = size(t)
                        need(sp, s_mid, t - 1)
                        sp.dma_start(xt[k][0:r, :], tile_rows(x, t, r)).then_inc(s_res[k], 16)
                        if not first:
                            sp.dma_start(x1t[k][0:r, :], tile_rows(x1_tab, t, r)).then_inc(s_res[k], 16)

                    def step(i, k):
                        if it := at(i, k, -1):
                            load_sums(*it)
                            load_residual(*it)
                        if not first and (it := at(i, k, LAGS)):
                            t, j, kk = it
                            r = size(t)
                            sp.wait_ge(s_out, t + 1)
                            sp.dma_start(tile_rows(out, t, r), OUT[kk][0:r, :]).then_inc(s_sa[kk], 16)
                    load_sums(0, 0, 0)
                    load_residual(0, 0, 0)
                    steps(sp, step)
                    for q in (s_sa, s_sb) if first else (s_sa,):
                        sp.wait_ge(q[0], 16 * (HALF + 1))
                        sp.wait_ge(q[1], 16 * HALF)

                @block.gpsimd
                def _(pool):
                    g_ = nc.gpsimd

                    def own_loop(t, j, k):
                        pool.wait_ge(s_in[k], 32 * (j + 1))
                        need(pool, s_nn, t - 1)
                        own = ES[:, bass.ds(t, 1), 0:nh].rearrange("p a h -> p (a h)")
                        g_.tensor_tensor(heads(B1[k][:]), heads(ht[k][:, 0:D]), spread(own), ALU.mult).then_inc(s_own, 1)

                    def affine(t, j, k):
                        pool.wait_ge(s_norm, t + 1)
                        g_.tensor_tensor(NM[k][:], NM[k][:], gain, ALU.mult).then_inc(s_pl, 1)
                        pool.wait_ge(s_pl, t + 1)
                        g_.tensor_tensor(Y[k][:], NM[k][:], shift, ALU.add).then_inc(s_y, 1)

                    def residual(t, j, k):
                        pool.wait_ge(s_res[k], 32 * (j + 1))
                        g_.tensor_tensor(xt[k][:], xt[k][:], x1t[k][:], ALU.add).then_inc(s_sum, 1)

                    def step(i, k):
                        if it := at(i, k, -1):
                            own_loop(*it)
                        if it := at(i, k, 0):
                            if not first:
                                residual(*it)
                            affine(*it)
                    own_loop(0, 0, 0)
                    steps(pool, step)

                NS = 5 + BN if nh == 1 else 6 + BN
                K_NEW = NS
                K_AFTER = 1 if first else 1 + BN
                K_GATE = 0 if first else 15
                KS = K_NEW + K_AFTER + K_GATE

                @block.vector
                def _(dve):
                    v = nc.vector

                    def new(st, t, j, k):
                        dve.wait_ge(s_in[k], 32 * (j + 1))
                        own = ES[:, bass.ds(t, 1), 0:nh].rearrange("p a h -> p (a h)")
                        st.link(v.tensor_tensor(small8[:, 0, 0:nh], own, ac[k][:, DEN:DEN + nh], ALU.add))
                        st.link(v.reciprocal(small8[:, 1, 0:nh], small8[:, 0, 0:nh]))
                        dve.wait_ge(s_own, t + 1)
                        st.link(v.tensor_tensor(B2[k][:], B1[k][:], ac[k][:, 0:D], ALU.add))
                        if nh == 1:
                            st.link(v.scalar_tensor_tensor(B2[k][:], B2[k][:], small8[:, 1, 0:1], bias, ALU.mult, ALU.add))
                        else:
                            st.link(v.tensor_tensor(heads(B2[k][:]), heads(B2[k][:]), spread(small8[:, 1, 0:nh]), ALU.mult))
                            st.link(v.tensor_tensor(B2[k][:], B2[k][:], bias, ALU.add))
                        mean, rstd, sh = bn_steps(st, B2[k][:], 0)
                        st.link(v.tensor_copy(smn[k][:, 0:1], rstd))
                        v.tensor_copy(smn[k][:, 1:2], sh).then_inc(s_nn, 1)

                    def after(st, t, j, k):
                        dve.wait_ge(s_el, t + 1)
                        st.link(v.scalar_tensor_tensor(NM[k][:], EX[k][:], -1.0, RP[k][:], ALU.add, ALU.add))
                        if first:
                            need(dve, s_sa[k], 16 * j)
                            v.tensor_tensor(X1[k][:], NM[k][:], XN[k][:], ALU.add).then_inc(s_mid, 1)
                            return
                        need(dve, s_out, t - 1)
                        dve.wait_ge(s_sum, t + 1)
                        v.tensor_tensor(X1[k][:], NM[k][:], xt[k][:], ALU.add).then_inc(s_mid, 1)
                        dve.wait_ge(s_mid, t + 1)
                        mean, rstd, sh = bn_steps(st, X1[k][:], 8)
                        v.tensor_copy(sm2[k][:, 0:1], rstd).then_inc(s_x2n, 1)
                        v.tensor_copy(sm2[k][:, 1:2], sh).then_inc(s_x2n, 1)

                    def gate(st, t, j, k):
                        dve.wait_ge(s_g, t + 1)
                        g = crep_ps[:, 0:NE]
                        st.link(v.tensor_reduce(sm[:, 16:17], g, AX.X, ALU.max))
                        v.tensor_scalar(g8[:, 0, :], g, sm[:, 16:17], None, ALU.subtract).then_inc(s_gz, 1)
                        dve.wait_ge(s_ge, t + 1)
                        st.link(v.tensor_reduce(sm[:, 17:18], g8[:, 1, :], AX.X, ALU.add))
                        st.link(v.reciprocal(sm[:, 18:19], sm[:, 17:18]))
                        st.link(v.tensor_scalar(g8[:, 2, :], g8[:, 1, :], sm[:, 18:19], None, ALU.mult))
                        sj = g8[:, 2:3, :].to_broadcast([P, NE, NE])
                        se = g8[:, 2, :].rearrange("p (e a) -> p e a", a=1).to_broadcast([P, NE, NE])
                        st.link(v.tensor_tensor(c3[0][:], sj, se, ALU.is_gt))
                        st.link(v.tensor_tensor(c3[1][:], sj, se, ALU.is_equal))
                        st.link(v.tensor_tensor(c3[2][:], c3[1][:], less[:], ALU.mult))
                        st.link(v.tensor_tensor(c3[1][:], c3[2][:], c3[0][:], ALU.add))
                        st.link(v.tensor_reduce(g8[:, 3, :], c3[1][:], AX.X, ALU.add))
                        st.link(v.tensor_scalar(g8[:, 4, :], g8[:, 3, :], 1.5, None, ALU.is_lt))
                        st.link(v.tensor_tensor(g8[:, 5, :], g8[:, 4, :], g8[:, 2, :], ALU.mult))
                        st.link(v.tensor_reduce(sm[:, 19:20], g8[:, 5, :], AX.X, ALU.add))
                        st.link(v.tensor_scalar(sm[:, 20:21], sm[:, 19:20], 1e-20, None, ALU.add))
                        st.link(v.reciprocal(sm[:, 21:22], sm[:, 20:21]))
                        need(dve, s_ct, t - 1)
                        st.link(v.memset(cw[k][:, NE:NE + 1], 1.0))
                        v.tensor_scalar(cw[k][:, 0:NE], g8[:, 5, :], sm[:, 21:22], None, ALU.mult).then_inc(s_cw, 1)

                    def weigh(t, g):
                        dve.wait_ge(s_relu, FG * t + g + 1)
                        dve.wait_ge(s_crep, (FG - 1) * t + g)
                        hv = hs[:, g % 2].rearrange("p j n -> p (j n)")
                        v.tensor_tensor(hv, hv, crep_ps[:], ALU.mult).then_inc(s_hs, 1)

                    def output(t, j, k):
                        dve.wait_ge(s_fo, t + 1)
                        need(dve, s_sa[k], 16 * j)
                        v.tensor_tensor(OUT[k][:], X1[k][:], dense_ps[:], ALU.add).then_inc(s_out, 1)

                    def step(i, k):
                        st = Steps(dve, s_v, (count[0] if isinstance(i, int) else KS * (2 * i + k - 4) + count[1]))
                        before, mid, late = at(i, k, 0), at(i, k, 1), None if first else at(i, k, 2)
                        if first and before:
                            new(st, *before)
                        if late:
                            weigh(late[0], 1)
                        if mid:
                            after(st, *mid)
                        if late:
                            weigh(late[0], 2)
                        if not first and before:
                            new(st, *before)
                        if late:
                            output(*late)
                        if mid and not first:
                            gate(st, *mid)
                        if isinstance(i, int):
                            count[0] += st.n
                            if (i, k) == (1, 1):
                                count[1] = count[0]
                                count[0] += KS * (NT - 7)
                        else:
                            assert st.n == KS, (st.n, KS)
                    count = [0, 0]
                    steps(dve, step)

                @block.scalar
                def _(act):
                    a_ = nc.scalar

                    def norm(t, j, k):
                        act.wait_ge(s_nn, t + 1)
                        a_.activation(NM[k][:], B2[k][:], ACT.Identity, bias=smn[k][:, 1:2], scale=smn[k][:, 0:1]).then_inc(s_norm, 1)

                    def elu(t, j, k):
                        act.wait_ge(s_y, t + 1)
                        a_.activation(RP[k][:], Y[k][:], ACT.Relu).then_inc(s_rp, 1)
                        a_.activation(B2[k][:], Y[k][:], ACT.Relu, scale=-1.0).then_inc(s_mr, 1)
                        act.wait_ge(s_mr, t + 1)
                        if first:
                            act.wait_ge(s_res[k], 16 * (j + 1))
                            sv = stats[:, bass.ds(t, 1), :].rearrange("p a k -> p (a k)")
                            a_.activation(XN[k][:], xt[k][:], ACT.Identity, bias=sv[:, 0:1], scale=sv[:, 1:2]).then_inc(s_xln, 1)
                        a_.activation(EX[k][:], B2[k][:], ACT.Exp, scale=-1.0).then_inc(s_el, 1)

                    def copy_t(t, j, k):
                        act.wait_ge(s_tp, t + 1)
                        a_.copy(xT[k][:], tr_ps[:].rearrange("p (k n) -> p k n", k=KT)).then_inc(s_tc, 1)

                    def copy_h(t, j, k):
                        act.wait_ge(s_mm, t + 1)
                        need(act, s_sb[k], 16 * j)
                        a_.copy(ho[k][:, 0:D], dense_ps[:])
                        a_.copy(ho[k][:, D:D + 1], small_ps[:, 0:1])
                        a_.copy(AS[:, bass.ds(t, 1), 0:1].rearrange("p a h -> p (a h)"), small_ps[:, 0:1])
                        a_.copy(AD[:, bass.ds(t, 1), 0:1].rearrange("p a h -> p (a h)"), small_ps[:, 1:2]).then_inc(s_ho, 1)
                        r = size(t)
                        act.wait_ge(s_mid, t + 1)
                        act.dma_start(tile_rows(x1_tab, t, r), X1[k][0:r, :]).then_inc(s_sa[k], 16)
                        act.wait_ge(s_ho, t + 1)
                        act.dma_start(tile_rows(h_tab[1], t, r), ho[k][0:r, :]).then_inc(s_sb[k], 16)

                    def norm2(t, j, k):
                        act.wait_ge(s_x2n, 2 * t + 2)
                        need(act, s_tp, t)
                        a_.activation(XL[:], X1[k][:], ACT.Identity, bias=sm2[k][:, 1:2], scale=sm2[k][:, 0:1]).then_inc(s_xl, 1)

                    def relus(t, g):
                        act.wait_ge(s_hid, FG * t + g + 1)
                        if g < 2:
                            need(act, s_fo if g == 0 else s_hs1, t)
                        else:
                            act.wait_ge(s_h0u, t + 1)
                        for q in range(4):
                            ins = a_.activation(hs[:, g % 2, q, :], (hid0_ps, hid1_ps)[g % 2][:, q * P:(q + 1) * P], ACT.Relu, bias=hb[:, 4 * g + q:4 * g + q + 1])
                        ins.then_inc(s_relu, 1)

                    def step(i, k):
                        before, mid, late = at(i, k, 0), at(i, k, 1), at(i, k, 2)
                        if not first:
                            if late:
                                relus(late[0], 0)
                                relus(late[0], 1)
                                act.wait_ge(s_ct, late[0] + 1)
                                a_.copy(ctr[late[2]][:], small_ps[0:NE + 1, 0:P]).then_inc(s_ctc, 1)
                            if mid:
                                elu(*mid)
                            if late:
                                relus(late[0], 2)
                            if mid:
                                norm2(*mid)
                                copy_t(*mid)
                            if before:
                                norm(*before)
                            if mid:
                                act.wait_ge(s_gz, mid[0] + 1)
                                a_.activation(g8[:, 1, :], g8[:, 0, :], ACT.Exp).then_inc(s_ge, 1)
                            return
                        if before:
                            norm(*before)
                            elu(*before)
                        if late:
                            copy_h(*late)
                        if mid:
                            copy_t(*mid)
                    if first:
                        for k in range(2):
                            a_.copy(ho[k][:, D:RW], ones[:, 0:8]).then_inc(s_ones, 1)
                        act.wait_ge(s_ones, 2)
                    steps(act, step)

                @block.tensor
                def _(pe):
                    m = nc.tensor

                    def turn(t, k):
                        src_t = X1[k] if first else XL
                        pe.wait_ge(s_mid if first else s_xl, t + 1)
                        need(pe, s_tc, t)
                        for j in range(KT):
                            ins = m.transpose(tr_ps[:, j * P:(j + 1) * P], src_t[:, j * P:(j + 1) * P], ident[:])
                        ins.then_inc(s_tp, 1)

                    def layer2(t, k):
                        pe.wait_ge(s_tc, t + 1)
                        need(pe, s_ho, t)
                        for j in range(KT):
                            m.matmul(dense_ps[:], xT[k][:, j, :], Wc[1][:, j, :], start=(j == 0), stop=(j == KT - 1))
                        for j in range(KT):
                            ins = m.matmul(small_ps[:, 0:2], xT[k][:, j, :], WA[1][:, j, 0:2], start=(j == 0), stop=(j == KT - 1))
                        ins.then_inc(s_mm, 1)

                    def hidden(t, k, g):
                        need(pe, s_relu, FG * t + (0 if g == 0 else -1 if g == 1 else 1))
                        for j in range(4):
                            for q in range(KT):
                                w = sw1_s[:, q, j * P:(j + 1) * P] if g == 0 else w1_s[:, q, 4 * (g - 1) + j, :]
                                ins = m.matmul((hid0_ps, hid1_ps)[g % 2][:, j * P:(j + 1) * P], w, xT[k][:, q, :], start=(q == 0), stop=(q == KT - 1), skip_group_check=True)
                        ins.then_inc(s_hid, 1)

                    def spread_weights(t, k, g):
                        if g == 1:
                            pe.wait_ge(s_ctc, t + 1)
                        else:
                            pe.wait_ge(s_hs, (FG - 1) * t + 1)
                        for j in range(4):
                            ins = m.matmul(crep_ps[:, j * P:(j + 1) * P], sel[:, 4 * (g - 1) + j, :], ctr[k][:], start=True, stop=True, skip_group_check=True)
                        ins.then_inc(s_crep, 1)

                    def output(t, g):
                        if g == 0:
                            pe.wait_ge(s_relu, FG * t + 1)
                            need(pe, s_out, t)
                        else:
                            pe.wait_ge(s_hs, (FG - 1) * t + g)
                        for j in range(4):
                            w = sw2_s[:, j, :] if g == 0 else w2_s[:, 4 * (g - 1) + j, :]
                            ins = m.matmul(dense_ps[:], hs[:, g % 2, j, :], w, start=(g == 0 and j == 0), stop=(g == 2 and j == 3))
                        ins.then_inc((s_h0u, s_hs1, s_fo)[g], 1)

                    def step(i, k):
                        before, mid, late = at(i, k, 0), at(i, k, 1), at(i, k, 2)
                        if first:
                            if late:
                                layer2(late[0], late[2])
                            if mid:
                                turn(mid[0], mid[2])
                            return
                        if late:
                            t, kk = late[0], late[2]
                            hidden(t, kk, 0)
                            hidden(t, kk, 1)
                            pe.wait_ge(s_cw, t + 1)
                            need(pe, s_ctc, t)
                            m.transpose(small_ps[0:NE + 1, 0:P], cw[kk][:, 0:NE + 1], ident[:]).then_inc(s_ct, 1)
                            output(t, 0)
                            spread_weights(t, kk, 1)
                            m.matmul(dense_ps[:], ctr[kk][:], b2c[:], start=False, stop=False)
                            hidden(t, kk, 2)
                            output(t, 1)
                            spread_weights(t, kk, 2)
                        if mid:
                            turn(mid[0], mid[2])
                        if late:
                            output(t, 2)
                        if mid:
                            t2, k2 = mid[0], mid[2]
                            pe.wait_ge(s_tc, t2 + 1)
                            if late:
                                pe.wait_ge(s_hs, (FG - 1) * t + 2)
                            for j in range(KT):
                                ins = m.matmul(crep_ps[:, 0:NE], xT[k2][:, j, :], gateT[:, j, :], start=(j == 0), stop=(j == KT - 1))
                            ins.then_inc(s_g, 1)
                    steps(pe, step)

        s_stats = sem("row_stats_made")
        with ExitStack() as ctx_stage:
            setup_stage()
        stages = [(project_stage,), (reference_stage, 0, H), (conv_stage, 0, H), (node_stage, 0, H),
                  (reference_stage, 1, 1), (conv_stage, 1, 1), (node_stage, 1, 1)]
        for stage, *args in stages:
            with ExitStack() as ctx_stage:
                def sbs(name, shape, dt=F32):
                    return ctx_stage.enter_context(nc.sbuf_tensor(name, shape, dt))
                stage(*args)


_INS = ["x", "src", "dst"] + ["L0_gnn_" + n for n in ("W1", "a_src1", "a_dst1", "b1", "g1", "beta1", "W2", "a_src2", "a_dst2", "b2", "g2", "beta2")] \
    + ["L0_ffn_" + n for n in ("gate_w", "w1", "b1", "w2", "b2", "sw1", "sb1", "sw2", "sb2")]


def kernel(**inputs):
    import numpy as _np
    import concourse.bacc as _bacc
    from concourse import mybir as _mybir
    from concourse.bass_utils import run_bass_kernel_spmd as _run

    nc = _bacc.Bacc("TRN2", target_bir_lowering=False, num_devices=1)
    arrays, args = {}, []
    for name in _INS:
        a = _np.ascontiguousarray(inputs[name])
        arrays[f"in_{name}_dram"] = a
        args.append(nc.dram_tensor(f"in_{name}_dram", a.shape, _mybir.dt.from_np(a.dtype), kind="ExternalInput").ap())
    shape = tuple(inputs["x"].shape)
    args.append(nc.dram_tensor("out_0_dram", shape, _mybir.dt.float32, kind="ExternalOutput").ap())
    gnn_ffn(nc, *args)
    r = _run(nc, [arrays], core_ids=[0])
    return r.results[0]["out_0_dram"]
```
